# Optimizing a Trainium2 kernel written in Bass

```python
import numpy as np
import jax
import jax.numpy as jnp

def _softmax(x, axis=-1):
    return jax.nn.softmax(x, axis=axis)

def _gelu(x):
    return jax.nn.gelu(x, approximate=True)

def _silu(x):
    return jax.nn.silu(x)

def _sigmoid(x):
    return jax.nn.sigmoid(x)

def _layernorm(x, axis=-1, eps=1e-05):
    m = jnp.mean(x, axis=axis, keepdims=True)
    v = jnp.var(x, axis=axis, keepdims=True)
    return (x - m) / jnp.sqrt(v + eps)

def _scatter_add(tgt, idx, src, axis=0):
    return tgt.at[idx].add(src)

def _segment_sum(src, seg, n):
    return jax.ops.segment_sum(src, seg, n)
kernel_name = 'mk_gnn_resnorm_d2_gnn_r64_321876'

def setup_inputs(seed: int=0):
    np.random.seed(seed)
    _w = jnp.asarray

    def _rec_inputs():
        import jax
        import jax.numpy as jnp
        _gk = jax.random.key(seed)
        x = -0.000202 + 1 * jax.random.normal(jax.random.fold_in(_gk, 1), (50000, 128), jnp.float32)
        src = jax.random.randint(jax.random.fold_in(_gk, 2), (25000,), 0, 50000, jnp.int32)
        dst = jnp.minimum((50000 * jax.random.uniform(jax.random.fold_in(_gk, 3), (25000,)) ** 2.0).astype(jnp.int32), 49999)
        _o = jnp.argsort(dst, stable=True)
        src = src[_o]
        dst = dst[_o]
        edge_attr_32 = 0.000196303 + 1.00016 * jax.random.normal(jax.random.fold_in(_gk, 11), (25000, 32), jnp.float32)
        return (x, src, dst, edge_attr_32)
    x, src, dst, edge_attr_32 = _rec_inputs()

    def _L0_gnn_setup():
        import jax, jax.numpy as jnp
        import numpy as np
        N_NODES = 50000
        N_EDGES = 12500
        NINP = 128
        D2 = 2 * NINP
        EPS = 1e-12

        def _l2norm(x):
            n = jnp.sqrt(jnp.sum(x * x, axis=-1, keepdims=True))
            return x / jnp.maximum(n, EPS)

        def _gcn_conv(x, W, b, src, dst, dinv):
            h = x @ W
            norm = dinv[src] * dinv[dst]
            agg = jax.ops.segment_sum(h[src] * norm[:, None], dst, num_segments=x.shape[0])
            agg = agg + (dinv * dinv)[:, None] * h
            return agg + b
        key = jax.random.key(seed)
        ks = jax.random.split(key, 11)
        s1 = 1.0 / np.sqrt(NINP)
        s2 = 1.0 / np.sqrt(D2)
        return {'node_embedding': jax.random.normal(ks[0], (N_NODES, NINP), jnp.float32), 'edge_index': jax.random.randint(ks[1], (2, N_EDGES), 0, N_NODES, dtype=jnp.int64), 'W1': jax.random.normal(ks[2], (NINP, D2), jnp.float32) * s1, 'b1': jnp.zeros((D2,), jnp.float32), 'Wf1': jax.random.normal(ks[3], (D2, D2), jnp.float32) * s2, 'bf1': jnp.zeros((D2,), jnp.float32), 'Wf2': jax.random.normal(ks[4], (D2, D2), jnp.float32) * s2, 'bf2': jnp.zeros((D2,), jnp.float32), 'W2': jax.random.normal(ks[5], (D2, NINP), jnp.float32) * s2, 'b2': jnp.zeros((NINP,), jnp.float32)}
    _L0_gnn_all = _L0_gnn_setup()
    _L0_gnn_in = {k: v for k, v in _L0_gnn_all.items() if k in ('W1', 'b1', 'Wf1', 'bf1', 'Wf2', 'bf2', 'W2', 'b2')}
    del _L0_gnn_all

    def _L1_gnn_setup():
        import jax, jax.numpy as jnp
        import numpy as np
        N, E = (50000, 12500)
        D_IN, HID, H, C, E_DIM = (128, 128, 4, 32, 32)
        key = jax.random.key(seed)
        ks = jax.random.split(key, 16)

        def lin(k, fan_in, fan_out):
            return jax.random.normal(k, (fan_in, fan_out), jnp.float32) / np.sqrt(fan_in)
        return {'x': jax.random.normal(ks[0], (N, D_IN), jnp.float32), 'edge_index': jax.random.randint(ks[1], (2, E), 0, N, jnp.int32), 'edge_attr': jax.random.normal(ks[2], (E, E_DIM), jnp.float32), 'Wq': lin(ks[3], D_IN, HID), 'bq': jnp.zeros((HID,), jnp.float32), 'Wk': lin(ks[4], D_IN, HID), 'bk': jnp.zeros((HID,), jnp.float32), 'Wv': lin(ks[5], D_IN, HID), 'bv': jnp.zeros((HID,), jnp.float32), 'We': lin(ks[6], E_DIM, HID), 'Wskip': lin(ks[7], D_IN, HID), 'bskip': jnp.zeros((HID,), jnp.float32), 'W1': lin(ks[8], HID, HID), 'b1': jnp.zeros((HID,), jnp.float32), 'W2': lin(ks[9], HID, HID), 'b2': jnp.zeros((HID,), jnp.float32)}
    _L1_gnn_all = _L1_gnn_setup()
    _L1_gnn_in = {k: v for k, v in _L1_gnn_all.items() if k in ('Wq', 'bq', 'Wk', 'bk', 'Wv', 'bv', 'We', 'Wskip', 'bskip', 'W1', 'b1', 'W2', 'b2')}
    del _L1_gnn_all
    return {'x': x, 'src': src, 'dst': dst, 'edge_attr_32': edge_attr_32, 'L0_gnn_W1': _L0_gnn_in['W1'], 'L0_gnn_b1': _L0_gnn_in['b1'], 'L0_gnn_Wf1': _L0_gnn_in['Wf1'], 'L0_gnn_bf1': _L0_gnn_in['bf1'], 'L0_gnn_Wf2': _L0_gnn_in['Wf2'], 'L0_gnn_bf2': _L0_gnn_in['bf2'], 'L0_gnn_W2': _L0_gnn_in['W2'], 'L0_gnn_b2': _L0_gnn_in['b2'], 'L1_gnn_Wq': _L1_gnn_in['Wq'], 'L1_gnn_bq': _L1_gnn_in['bq'], 'L1_gnn_Wk': _L1_gnn_in['Wk'], 'L1_gnn_bk': _L1_gnn_in['bk'], 'L1_gnn_Wv': _L1_gnn_in['Wv'], 'L1_gnn_bv': _L1_gnn_in['bv'], 'L1_gnn_We': _L1_gnn_in['We'], 'L1_gnn_Wskip': _L1_gnn_in['Wskip'], 'L1_gnn_bskip': _L1_gnn_in['bskip'], 'L1_gnn_W1': _L1_gnn_in['W1'], 'L1_gnn_b1': _L1_gnn_in['b1'], 'L1_gnn_W2': _L1_gnn_in['W2'], 'L1_gnn_b2': _L1_gnn_in['b2']}

def reference(x, src, dst, edge_attr_32, L0_gnn_W1, L0_gnn_b1, L0_gnn_Wf1, L0_gnn_bf1, L0_gnn_Wf2, L0_gnn_bf2, L0_gnn_W2, L0_gnn_b2, L1_gnn_Wq, L1_gnn_bq, L1_gnn_Wk, L1_gnn_bk, L1_gnn_Wv, L1_gnn_bv, L1_gnn_We, L1_gnn_Wskip, L1_gnn_bskip, L1_gnn_W1, L1_gnn_b1, L1_gnn_W2, L1_gnn_b2):
    import jax
    import jax.numpy as jnp

    def _L0_gnn_ref(node_embedding, edge_index, W1, b1, Wf1, bf1, Wf2, bf2, W2, b2):
        import jax, jax.numpy as jnp
        import numpy as np
        N_NODES = 50000
        N_EDGES = 12500
        NINP = 128
        D2 = 2 * NINP
        EPS = 1e-12

        def _l2norm(x):
            n = jnp.sqrt(jnp.sum(x * x, axis=-1, keepdims=True))
            return x / jnp.maximum(n, EPS)

        def _gcn_conv(x, W, b, src, dst, dinv):
            h = x @ W
            norm = dinv[src] * dinv[dst]
            agg = jax.ops.segment_sum(h[src] * norm[:, None], dst, num_segments=x.shape[0])
            agg = agg + (dinv * dinv)[:, None] * h
            return agg + b
        src, dst = (edge_index[0], edge_index[1])
        n = node_embedding.shape[0]
        deg = jax.ops.segment_sum(jnp.ones(src.shape[0], node_embedding.dtype), dst, num_segments=n) + 1.0
        dinv = jax.lax.rsqrt(deg)
        x = _gcn_conv(node_embedding, W1, b1, src, dst, dinv)
        x = _l2norm(x)

        def f(z):
            z1 = _gcn_conv(z, Wf1, bf1, src, dst, dinv)
            z1 = _l2norm(z1)
            return _gcn_conv(z1, Wf2, bf2, src, dst, dinv) + z
        k1 = f(x)
        k2 = f(x + 0.5 * k1)
        k3 = f(x + 0.5 * k2)
        k4 = f(x + k3)
        x = x + (k1 + 2.0 * k2 + 2.0 * k3 + k4) / 6.0
        return _gcn_conv(x, W2, b2, src, dst, dinv)

    def _L1_gnn_ref(x, edge_index, edge_attr, Wq, bq, Wk, bk, Wv, bv, We, Wskip, bskip, W1, b1, W2, b2):
        import jax, jax.numpy as jnp
        import numpy as np
        N, E = (50000, 12500)
        D_IN, HID, H, C, E_DIM = (128, 128, 4, 32, 32)
        src, dst = (edge_index[0], edge_index[1])
        n = x.shape[0]
        q = (x @ Wq + bq).reshape(n, H, C)
        k = (x @ Wk + bk).reshape(n, H, C)
        v = (x @ Wv + bv).reshape(n, H, C)
        e = (edge_attr @ We).reshape(-1, H, C)
        kj = k[src] + e
        vj = v[src] + e
        alpha = jnp.einsum('ehc,ehc->eh', q[dst], kj) / np.sqrt(C)
        amax = jax.ops.segment_max(alpha, dst, num_segments=n)
        amax = jnp.where(jnp.isfinite(amax), amax, 0.0)
        ex = jnp.exp(alpha - amax[dst])
        denom = jax.ops.segment_sum(ex, dst, num_segments=n)
        alpha = ex / (denom[dst] + 1e-16)
        agg = jax.ops.segment_sum(vj * alpha[:, :, None], dst, num_segments=n)
        out = agg.reshape(n, HID) + (x @ Wskip + bskip)
        h = jax.nn.gelu(out @ W1 + b1, approximate=True)
        h = jax.nn.gelu(h @ W2 + b2, approximate=True)
        return out + h
    edge_index = jnp.stack([src, dst])
    x = _layernorm(x + _L0_gnn_ref(x, edge_index, L0_gnn_W1, L0_gnn_b1, L0_gnn_Wf1, L0_gnn_bf1, L0_gnn_Wf2, L0_gnn_bf2, L0_gnn_W2, L0_gnn_b2), axis=-1)
    x = _layernorm(x + _L1_gnn_ref(x, edge_index, edge_attr_32, L1_gnn_Wq, L1_gnn_bq, L1_gnn_Wk, L1_gnn_bk, L1_gnn_Wv, L1_gnn_bv, L1_gnn_We, L1_gnn_Wskip, L1_gnn_bskip, L1_gnn_W1, L1_gnn_b1, L1_gnn_W2, L1_gnn_b2), axis=-1)
    return x

_drawn_inputs = setup_inputs


def setup_inputs(seed=0):
    import zlib

    import numpy as np

    out = dict(_drawn_inputs(seed))
    spreads = {'L0_gnn_b1': (0.0, 0.364),
     'L0_gnn_bf1': (0.0, 0.1),
     'L0_gnn_bf2': (0.0, 0.1),
     'L0_gnn_b2': (0.0, 0.1),
     'L1_gnn_bq': (0.0, 0.731),
     'L1_gnn_bk': (0.0, 0.8),
     'L1_gnn_bv': (0.0, 0.1),
     'L1_gnn_bskip': (0.0, 0.1),
     'L1_gnn_b1': (0.0, 0.308),
     'L1_gnn_b2': (0.0, 0.1)}
    factors = {}
    for name, (base, spread) in spreads.items():
        noise = np.random.default_rng([zlib.crc32(name.encode()), seed]).standard_normal(out[name].shape)
        drawn = base * np.exp(spread * noise) if base else spread * noise
        out[name] = jnp.asarray(drawn.astype(out[name].dtype))
    for name, factor in factors.items():
        out[name] = (out[name] * factor).astype(out[name].dtype)
    return out
```

```python
import concourse.bass as bass
from concourse import mybir

F32 = mybir.dt.float32
F32R = mybir.dt.float32r
BF16 = mybir.dt.bfloat16
I32 = mybir.dt.int32
ALU = mybir.AluOpType
ACT = mybir.ActivationFunctionType
AX = mybir.AxisListType

P = 128
NODES, EDGES = 50000, 25000
D, H2 = 128, 256
HEADS, HC, ED = 4, 32, 32
TE = -(-EDGES // P)
TL = -(-(-(-NODES // P) - TE) // 8) * 8
TN = TE + TL
SLOTS, NPAD = TE * P, TN * P
FILL = NPAD
XW = D + 2
NONE = 1 << 28
L2_EPS, LN_EPS, DEN_EPS = 1e-12, 1e-5, 1e-16
NEG = -3.0e38
RK = (0.5, 0.5, 1.0)


def skewed(eng, count, steps, ring=4):
    most = max(lag for lag, _ in steps)
    head = -(-(most + ring) // ring) * ring
    turns = (count - head) // ring

    def turn(t, residue):
        for lag, body in steps:
            j = t - lag
            if not isinstance(j, int) or 0 <= j < count:
                body(j, (residue - lag) % ring)

    if turns < 1:
        for t in range(count + most):
            turn(t, t % ring)
        return
    for t in range(head):
        turn(t, t % ring)
    end = head + ring * turns
    with eng.Fori(head, end - ring + 1, ring) as i:
        for c in range(ring):
            turn(i + c, c)
    for t in range(end, count + most):
        turn(t, t % ring)


def pool_wait(pool, sem, value, apart):
    pool.wait_ge(sem, value)
    if not isinstance(value, int):
        pool.sem_inc(apart, 1)


class Counts:

    def __init__(self):
        self.total = {}

    def phase(self, count, rates, ring=4):
        return Phase(self, count, rates, ring)


class Phase:
    def __init__(self, counts, count, rates, ring):
        self.counts, self.count, self.ring = counts, count, ring
        self.rate = {name: n for name, n in rates.items() if n}
        self.base = dict(counts.total)
        for name, n in self.rate.items():
            if name.endswith("*"):
                for s in range(ring):
                    uses = len(range(s, count, ring))
                    counts.total[name[:-1] + str(s)] = counts.total.get(name[:-1] + str(s), 0) + n * uses
            else:
                counts.total[name] = counts.total.get(name, 0) + n * count

    def at(self, name, j, n=None):
        rate = self.rate[name]
        return j * rate + (self.base.get(name, 0) + (rate if n is None else n))

    def ring_at(self, name, j, s, back=0):
        rate = self.rate[name + "*"]
        return (j - s) * (rate // self.ring) + (self.base.get(name + str(s), 0) + rate * (1 - back))

    def end(self, name):
        return self.counts_at_end(name)

    def counts_at_end(self, name):
        return self.base.get(name, 0) + self.rate[name] * self.count

    def ring_end(self, name, s):
        return self.base.get(name + str(s), 0) + self.rate[name + "*"] * len(range(s, self.count, self.ring))


def skewed_blocks(eng, blocks, size, steps):
    def turn(b, q):
        for lag, body in steps:
            if q >= lag:
                if not isinstance(b, int) or b < blocks:
                    body(b, q - lag)
            elif not isinstance(b, int) or b > 0:
                body(b - 1, q - lag + size)

    for b in range(2):
        for q in range(size):
            turn(b, q)
    with eng.Fori(2, blocks) as b:
        for q in range(size):
            turn(b, q)
    for q in range(max(lag for lag, _ in steps)):
        turn(blocks, q)


class BlockPhase:

    def __init__(self, counts, blocks, rates):
        self.base, self.rates, self.blocks = dict(counts.total), rates, blocks
        for name, r in rates.items():
            counts.total[name] = counts.total.get(name, 0) + blocks * sum(r)

    def at(self, name, b, q, n=None):
        r = self.rates[name]
        return b * sum(r) + (self.base.get(name, 0) + sum(r[:q]) + (r[q] if n is None else n))

    def end(self, name):
        return self.base.get(name, 0) + self.blocks * sum(self.rates[name])


def gnn_kernel(nc, a, out):
    tensors = {}

    def sb(name, shape, dt=F32):
        return nc.alloc_sbuf_tensor(name, list(shape), dt)

    def dram(name, shape, dt=F32):
        return nc.dram_tensor(name, list(shape), dt, kind="Internal").ap()

    class Sems(dict):
        def __missing__(self, name):
            self[name] = nc.alloc_semaphore(name)
            return self[name]

    S = Sems()
    counts = Counts()

    x_tab = dram("x_tab", [NPAD + SLOTS, XW])
    pos_tab = dram("pos_tab", [NPAD, 1], I32)
    free_tab = dram("free_tab", [SLOTS, 1], I32)
    sum_tab = dram("sum_tab", [TE, P, P])
    z_tab = [dram(f"z{i}_tab", [NPAD, H2]) for i in range(4)]
    t_tab = [dram(f"t{i}_tab", [NPAD, H2]) for i in range(4)]
    xf_tab = dram("xf_tab", [NPAD, H2])
    x1_tab = dram("x1_tab", [NPAD, D])
    v_tab = dram("v_tab", [SLOTS, D])
    agg_tab = dram("agg_tab", [SLOTS, D])
    alpha_line = dram("alpha_line", [HEADS, SLOTS])
    max_line = dram("max_line", [HEADS, SLOTS])
    xo_tab = dram("xo_tab", [SLOTS, D])

    ident = sb("ident", [P, P])
    lead = sb("lead", [P, TE])
    carry = sb("carry", [P, TE])
    own_row = sb("own_row", [P, TE], I32)
    src_row1 = sb("src_row1", [P, TE], I32)
    src_row = sb("src_row", [P, TE], I32)
    dst_row = sb("dst_row", [P, TE], I32)
    dinv = sb("dinv", [P, TE])
    node_of = sb("node_of", [P, TN], I32)
    src_i = sb("src_i", [P, TE], I32)
    dst_i = sb("dst_i", [P, TE], I32)
    zero_i = sb("zero_i", [P, TE], I32)
    free_i = sb("free_i", [P, TE], I32)
    slot_id_i = sb("slot_id_i", [P, TE], I32)
    node_pos = sb("node_pos", [P, TN], I32)
    for name, ks, width in (("w1", 1, H2), ("wf1", 2, H2), ("wf2", 2, H2), ("w2", 2, D)):
        tensors[name + "_hi"] = sb(name + "_hi", [P, ks, width], F32R)
        tensors[name + "_lo"] = sb(name + "_lo", [P, ks, width], F32R)
    for name, width in (("b1", H2), ("bf1", H2), ("bf2", H2), ("b2", D)) + tuple((f"bf2_{r}", H2) for r in range(4)):
        tensors[name] = sb(name, [P, width])
    ones_r = sb("ones_r", [P, P], F32R)
    bf2_parts = sb("bf2_parts", [P, H2], F32R)
    psum = [nc.alloc_psum_tensor(f"bank{i}", [P, 512], F32) for i in range(8)]

    m = dict(locals(), **tensors)
    prepare(nc, a, S, counts, m)
    local_pass(nc, a, S, counts, m)
    if a.get("stop") == "local":
        return m
    coupled_stages(nc, a, S, counts, m)
    if a.get("stop") == "coupled":
        return m
    attention(nc, a, S, counts, m)
    return m


def prepare(nc, a, S, counts, m):
    ident, lead, carry, psum = m["ident"], m["lead"], m["carry"], m["psum"]
    from contextlib import ExitStack
    ctx = ExitStack()

    def sb(name, shape, dt=F32):
        return ctx.enter_context(nc.sbuf_tensor(name, list(shape), dt))

    with ctx:
        src_i, dst_i, free_i, slot_id_i = m["src_i"], m["dst_i"], m["free_i"], m["slot_id_i"]
        next_i = sb("next_i", [P, TE], I32)
        part_i = sb("part_i", [P, TE], I32)
        dst_f = sb("dst_f", [P, TE])
        next_f = sb("next_f", [P, TE])
        dst_hi = sb("dst_hi", [P, TE])
        dst_lo = sb("dst_lo", [P, TE])
        lead_tile = sb("lead_tile", [P, TE])
        lead_part = sb("lead_part", [P, TE])
        follow = sb("follow", [P, TE])
        cols = sb("cols", [P, TN])
        part = sb("part", [P, 1])
        zeros = sb("zeros", [P, XW])
        ones = sb("ones", [P, P])
        up = sb("up", [P, P])
        down = sb("down", [P, P])
        above = sb("above", [P, P])
        hot_hi = sb("hot_hi", [P, 4, TN], BF16)
        hot_lo = sb("hot_lo", [P, 4, 3, P], BF16)
        rows_i = sb("rows_i", [P, 2, 4 * P], I32)
        rows_f = sb("rows_f", [P, 2, 4 * P])
        sums = sb("sums", [P, 2, 4, P])
        deg = sb("deg", [P, TN])
        slot = sb("slot", [P, TN])
        alone = sb("alone", [P, TN])
        rank = sb("rank", [P, TN])
        tmp = sb("tmp", [P, TN])
        tmp2 = sb("tmp2", [P, TN])
        scan = sb("scan", [P, TN])
        pos_f = sb("pos_f", [P, TN])
        node_f = sb("node_f", [P, TN])
        node_dinv = sb("node_dinv", [P, TN])
        fill_rank = sb("fill_rank", [P, TE])
        slot_id = sb("slot_id", [P, TE])
        pos_rows = sb("pos_rows", [P, 4, P], I32)
        hot_deg, hot_tile, hot_part = psum[0], psum[1], psum[2]

        turns = TE // 4
        ph = counts.phase(turns, {"sums_in*": 16, "row_floats": 1, "sums_built": 1, "stored*": 16,
                                  "hot": 4, "counted": 4}, ring=2)
        NV = [0]

        with nc.Block() as block:
            @block.sync
            def _(sp):
                sp.dma_start(dst_i[:], a["dst"]).then_inc(S["edges_in"], 16)
                sp.dma_start(next_i[:], a["dst_next"]).then_inc(S["edges_in"], 16)
                sp.dma_start(src_i[:], a["src"]).then_inc(S["edges_in"], 16)
                sp.wait_ge(S["zeros"], 2)
                for lo in (0, FILL):
                    sp.dma_start(m["x_tab"][lo:lo + SLOTS, :].rearrange("(p n) c -> p n c", p=P),
                                 zeros[:].unsqueeze(1).to_broadcast([P, TE, XW])).then_inc(S["cleared"], 16)
                sp.dma_start(m["free_tab"].rearrange("(p n) c -> p (n c)", p=P), m["zero_i"][:]
                             ).then_inc(S["cleared"], 16)

                def rows(j, s):
                    if not isinstance(j, int) or j >= 2:
                        sp.wait_ge(S["row_floats"], ph.at("row_floats", j - 2))
                    sp.dma_start(rows_i[:, s, :], a["dst_rows"][bass.ds(j * (4 * P), 4 * P)].partition_broadcast(P)
                                 ).then_inc(S["sums_in%d" % s], 16)

                def store(j, s):
                    sp.wait_ge(S["sums_built"], ph.at("sums_built", j))
                    sp.dma_start(m["sum_tab"][bass.ds(j * 4, 4), :, :].rearrange("t p f -> p t f"),
                                 sums[:, s, :, :]).then_inc(S["stored%d" % s], 16)
                skewed(sp, turns, [(0, rows), (1, store)], ring=2)
                for s in range(2):
                    sp.wait_ge(S["stored%d" % s], ph.ring_end("stored", s))
                sp.wait_ge(S["cleared"], 48)

            @block.gpsimd
            def _(pool):
                nc.gpsimd.memset(zeros[:], 0.0).then_inc(S["zeros"], 1)
                nc.gpsimd.memset(m["zero_i"][:], 0).then_inc(S["zeros"], 1)
                nc.gpsimd.memset(ones[:], 1.0).then_inc(S["filled"], 1)
                nc.gpsimd.memset(ident[:], 0.0).then_inc(S["filled"], 1)
                nc.gpsimd.iota(cols[:], [[1, TN]], base=0, channel_multiplier=0,
                               allow_small_or_imprecise_dtypes=True).then_inc(S["masks"], 1)
                nc.gpsimd.iota(part[:], [[0, 1]], base=0, channel_multiplier=1,
                               allow_small_or_imprecise_dtypes=True).then_inc(S["masks"], 1)
                nc.gpsimd.iota(node_f[:], [[P, TN]], base=0, channel_multiplier=1,
                               allow_small_or_imprecise_dtypes=True).then_inc(S["masks"], 1)
                pool.wait_ge(S["filled"], 2)
                nc.gpsimd.affine_select(ident[:], ident[:], [[-1, P]], ALU.not_equal, 1.0, base=0,
                                        channel_multiplier=1).then_inc(S["masks"], 1)
                nc.gpsimd.affine_select(up[:], ones[:], [[1, P]], ALU.is_ge, 0.0, base=0,
                                        channel_multiplier=-1).then_inc(S["masks"], 1)
                nc.gpsimd.affine_select(down[:], ones[:], [[-1, P]], ALU.is_ge, 0.0, base=0,
                                        channel_multiplier=1).then_inc(S["masks"], 1)
                nc.gpsimd.affine_select(above[:], ones[:], [[1, P]], ALU.is_ge, 0.0, base=-1,
                                        channel_multiplier=-1).then_inc(S["masks"], 1)

            @block.vector
            def _(dve):
                def link(ins):
                    NV[0] += 1
                    ins.then_inc(S["linked"], 1)
                    dve.wait_ge(S["linked"], NV[0])

                dve.wait_ge(S["edges_in"], 48)
                dve.wait_ge(S["masks"], 7)
                v = nc.vector
                v.tensor_copy(dst_f[:], dst_i[:])
                v.tensor_scalar(part_i[:], dst_i[:], 7, None, ALU.logical_shift_right)
                link(v.tensor_copy(next_f[:], next_i[:]))
                v.tensor_tensor(lead[:], dst_f[:], next_f[:], ALU.not_equal)
                link(v.tensor_copy(dst_hi[:], part_i[:]))
                link(v.tensor_scalar(part_i[:], dst_i[:], P - 1, None, ALU.bitwise_and))
                v.tensor_copy(dst_lo[:], part_i[:])
                v.tensor_tensor(lead_tile[:], lead[:], cols[:, 0:TE], ALU.mult)
                v.tensor_scalar(lead_part[:], lead[:], part[:, 0:1], None, ALU.mult)
                v.tensor_scalar(follow[:], lead[:], -1.0, 1.0, ALU.mult, ALU.add)
                link(v.memset(carry[:], 0.0))
                link(v.tensor_tensor(carry[:, 1:TE], dst_f[:, 1:TE], dst_f[:, 0:TE - 1], ALU.is_equal))
                cv = carry[:].rearrange("p (t i) -> p t i", i=2)
                link(v.tensor_scalar(cv[:, :, 0], cv[:, :, 0], ident[:, 0:1], None, ALU.mult))
                link(v.tensor_scalar(cv[:, :, 1], cv[:, :, 1], ident[:, P - 1:P], None, ALU.mult))

                def floats(j, s):
                    dve.wait_ge(S["sums_in%d" % s], ph.ring_at("sums_in", j, s))
                    if not isinstance(j, int) or j >= 2:
                        dve.wait_ge(S["stored%d" % s], ph.ring_at("stored", j, s, back=1))
                    v.tensor_copy(rows_f[:, s, :], rows_i[:, s, :]).then_inc(S["row_floats"], 1)
                    dve.wait_ge(S["row_floats"], ph.at("row_floats", j))
                    for i in range(4):
                        last = v.scalar_tensor_tensor(sums[:, s, i, :], rows_f[:, s, i * P:(i + 1) * P],
                                                      dst_f[:, bass.ds(j * 4 + i, 1)], (up, down)[i % 2][:],
                                                      ALU.is_equal, ALU.mult)
                    last.then_inc(S["sums_built"], 1)

                def hots(j, s):
                    for i in range(4):
                        if not isinstance(j, int) or j >= 1:
                            dve.wait_ge(S["counted"], ph.at("counted", j - 1, i + 1))
                        t = bass.ds(j * 4 + i, 1)
                        v.tensor_scalar(hot_hi[:, i, :], cols[:], dst_hi[:, t], None, ALU.is_equal)
                        v.tensor_scalar(hot_lo[:, i, 0, :], cols[:, 0:P], dst_lo[:, t], None, ALU.is_equal)
                        v.tensor_scalar(hot_lo[:, i, 1, :], cols[:, 0:P], dst_lo[:, t], lead_tile[:, t],
                                        ALU.is_equal, ALU.mult)
                        v.tensor_scalar(hot_lo[:, i, 2, :], cols[:, 0:P], dst_lo[:, t], lead_part[:, t],
                                        ALU.is_equal, ALU.mult).then_inc(S["hot"], 1)
                skewed(dve, turns, [(0, floats), (0, hots)], ring=2)

            @block.tensor
            def _(pe):
                def count(j, s):
                    for i in range(4):
                        pe.wait_ge(S["hot"], ph.at("hot", j, i + 1))
                        first = isinstance(j, int) and j == 0 and i == 0
                        last_ = isinstance(j, int) and j == turns - 1 and i == 3
                        for k in range(3):
                            last = nc.tensor.matmul(psum[k][:, 0:TN], hot_lo[:, i, k, :], hot_hi[:, i, :],
                                                    start=first, stop=last_)
                        last.then_inc(S["counted"], 1)
                skewed(pe, turns, [(0, count), (1, lambda j, s: None)], ring=2)

        with nc.Block() as block:
            @block.vector
            def _(dve):
                v = nc.vector

                def link(ins):
                    NV[0] += 1
                    ins.then_inc(S["linked"], 1)
                    dve.wait_ge(S["linked"], NV[0])

                v.tensor_copy(deg[:], hot_deg[:, 0:TN])
                v.tensor_copy(tmp[:], hot_part[:, 0:TN])
                link(v.tensor_scalar(slot[:], hot_tile[:, 0:TN], float(P), None, ALU.mult))
                link(v.tensor_tensor(slot[:], slot[:], tmp[:], ALU.add))
                link(v.tensor_scalar(alone[:], deg[:], 0.0, None, ALU.is_equal))
                link(v.tensor_scalar(node_dinv[:], deg[:], 1.0, None, ALU.add))
                v.tensor_copy(tmp[:], tmp[:]).then_inc(S["alone"], 1)

                def prefix(vec, width, name, total_psum, within_psum, res):
                    dve.wait_ge(S[name], 1)
                    link(v.memset(tmp2[:], 0.0))
                    link(v.tensor_copy(tmp[:, 0:width], total_psum[:, 0:width]))
                    link(v.tensor_tensor_scan(scan[:, 0:width], tmp[:, 0:width], tmp2[:, 0:width], 0.0,
                                              ALU.add, ALU.add))
                    link(v.tensor_tensor(res[:], within_psum[:, 0:width], scan[:, 0:width], ALU.add))
                    link(v.tensor_tensor(res[:], res[:], tmp[:, 0:width], ALU.subtract))

                prefix(follow, TE, "free_sums", psum[3], psum[4], fill_rank)
                link(v.tensor_scalar(slot_id[:], cols[:, 0:TE], float(P), part[:, 0:1], ALU.mult, ALU.add))
                link(v.tensor_copy(slot_id_i[:], slot_id[:]))
                link(v.tensor_scalar(tmp[:, 0:TE], fill_rank[:], float(FILL), None, ALU.add))
                link(v.tensor_tensor(tmp[:, 0:TE], tmp[:, 0:TE], slot_id[:], ALU.subtract))
                link(v.tensor_tensor(tmp[:, 0:TE], tmp[:, 0:TE], follow[:], ALU.mult))
                link(v.tensor_tensor(tmp[:, 0:TE], tmp[:, 0:TE], slot_id[:], ALU.add))
                link(v.tensor_copy(m["own_row"][:], tmp[:, 0:TE]))
                link(v.tensor_scalar(tmp[:, 0:TE], lead[:], float(NONE), None, ALU.mult))
                link(v.tensor_tensor(tmp[:, 0:TE], tmp[:, 0:TE], fill_rank[:], ALU.add))
                link(v.tensor_copy(free_i[:], tmp[:, 0:TE]))

                prefix(alone, TN, "alone_sums", psum[5], psum[6], rank)
                link(v.tensor_scalar(tmp[:, 0:1], scan[:, TN - 1:TN], float(-TL * P), None, ALU.add))
                link(v.tensor_scalar(tmp2[:], rank[:], tmp[:, 0:1], None, ALU.is_lt))
                link(v.tensor_scalar(tmp[:, 1:2], tmp[:, 0:1], -1.0, float(SLOTS), ALU.mult, ALU.add))
                link(v.tensor_scalar(tmp[:, 2:3], tmp[:, 1:2], -1.0, float(FILL), ALU.mult, ALU.add))
                link(v.tensor_scalar(tmp2[:], tmp2[:], tmp[:, 2:3], tmp[:, 1:2], ALU.mult, ALU.add))
                link(v.tensor_tensor(tmp2[:], tmp2[:], rank[:], ALU.add))
                link(v.tensor_tensor(tmp2[:], tmp2[:], alone[:], ALU.mult))
                link(v.tensor_tensor(pos_f[:], tmp2[:], slot[:], ALU.add))
                v.tensor_copy(m["node_pos"][:], pos_f[:]).then_inc(S["positions"], 1)
                dve.wait_ge(S["root"], 1)
                link(v.reciprocal(tmp[:], rank[:]))
                link(v.tensor_tensor(tmp2[:], tmp[:], tmp[:], ALU.mult))
                link(v.tensor_tensor(tmp2[:], tmp2[:], node_dinv[:], ALU.mult))
                link(v.tensor_scalar(tmp2[:], tmp2[:], -0.5, 1.5, ALU.mult, ALU.add))
                link(v.tensor_tensor(node_dinv[:], tmp2[:], tmp[:], ALU.mult))
                dve.wait_ge(S["pos_turned"], 4)
                for k in range(4):
                    last = v.tensor_copy(pos_rows[0:TN // 4, k, :], psum[7][0:TN // 4, k * P:(k + 1) * P])
                last.then_inc(S["pos_rows"], 1)

            @block.scalar
            def _(act):
                act.wait_ge(S["positions"], 1)
                nc.scalar.activation(rank[:], node_dinv[:], ACT.Sqrt).then_inc(S["root"], 1)

            @block.tensor
            def _(pe):
                nc.tensor.matmul(psum[3][:, 0:TE], ones[:], follow[:], start=True, stop=True)
                nc.tensor.matmul(psum[4][:, 0:TE], above[:], follow[:], start=True, stop=True
                                 ).then_inc(S["free_sums"], 1)
                pe.wait_ge(S["alone"], 1)
                nc.tensor.matmul(psum[5][:, 0:TN], ones[:], alone[:], start=True, stop=True)
                nc.tensor.matmul(psum[6][:, 0:TN], above[:], alone[:], start=True, stop=True
                                 ).then_inc(S["alone_sums"], 1)
                pe.wait_ge(S["positions"], 1)
                for k in range(4):
                    w = TN // 4
                    nc.tensor.transpose(psum[7][0:w, k * P:(k + 1) * P], pos_f[:, k * w:(k + 1) * w],
                                        ident[:]).then_inc(S["pos_turned"], 1)

            @block.sync
            def _(sp):
                sp.wait_ge(S["pos_rows"], 1)
                w = TN // 4
                sp.dma_start(m["pos_tab"].rearrange("(k h l) o -> h k (l o)", k=4, h=w), pos_rows[0:w, :, :]
                             ).then_inc(S["pos_out"], 16)
                sp.wait_ge(S["pos_out"], 16)

        x_in = sb("x_in", [P, 4, 4, XW])
        stage_pos = sb("stage_pos", [P, 4, 4], I32)
        turns = TN // 4
        px = counts.phase(turns, {"own_in*": 16, "x_row": 1, "x_row_pos": 1, "scattered*": 64})
        with nc.Block() as block:
            @block.sync
            def _(sp):
                def load(j, s):
                    if not isinstance(j, int) or j >= 4:
                        sp.wait_ge(S["scattered%d" % s], px.ring_at("scattered", j, s, back=1))
                    sp.dma_start(x_in[:, s, :, 0:D], a["x"].rearrange("(t p) c -> p t c", p=P)[:, bass.ds(j * 4, 4), :]
                                 ).then_inc(S["own_in%d" % s], 16)
                skewed(sp, turns, [(0, load)])

            @block.vector
            def _(dve):
                def fill(j, s):
                    if not isinstance(j, int) or j >= 4:
                        dve.wait_ge(S["scattered%d" % s], px.ring_at("scattered", j, s, back=1))
                    nc.vector.tensor_copy(stage_pos[:, s, :], m["node_pos"][:, bass.ds(j * 4, 4)])
                    nc.vector.tensor_copy(x_in[:, s, :, D], node_f[:, bass.ds(j * 4, 4)])
                    nc.vector.tensor_copy(x_in[:, s, :, D + 1], node_dinv[:, bass.ds(j * 4, 4)]
                                          ).then_inc(S["x_row"], 1)
                skewed(dve, turns, [(0, fill)])

            @block.gpsimd
            def _(pool):
                def scatter(j, s):
                    pool_wait(pool, S["x_row"], px.at("x_row", j), S["apart"])
                    pool_wait(pool, S["own_in%d" % s], px.ring_at("own_in", j, s), S["apart"])
                    for i in range(4):
                        pool.indirect_dma_start(
                            out=m["x_tab"], out_offset=bass.IndirectOffsetOnAxis(ap=stage_pos[:, s, i:i + 1], axis=0),
                            in_=x_in[:, s, i, :], in_offset=None).then_inc(S["scattered%d" % s], 16)
                skewed(pool, turns, [(0, scatter)])
                for s in range(4):
                    pool.wait_ge(S["scattered%d" % s], px.ring_end("scattered", s))


def edge_tables(nc, S, counts, m, pool):
    stage_a, stage_b, got = m["stage_a"], m["stage_b"], m["got"]
    free_i = m["free_i"]
    g = nc.gpsimd
    turns = TE // 4

    def gather(index, table, result, bound, prefill=None):
        pg = counts.phase(turns, {"index_set": 1, "gathered*": 64, "kept": 1}, ring=2)

        def ask(j, s):
            if not isinstance(j, int) or j >= 2:
                pool_wait(pool, S["kept"], pg.at("kept", j - 2), S["apart"])
            if prefill is not None:
                g.tensor_copy(got[:, s, :], prefill[:, bass.ds(j * 4, 4)])
            g.tensor_copy(stage_a[:, s, :], index[:, bass.ds(j * 4, 4)]).then_inc(S["index_set"], 1)
            pool_wait(pool, S["index_set"], pg.at("index_set", j), S["apart"])
            for i in range(4):
                pool.indirect_dma_start(
                    out=got[:, s, i:i + 1], out_offset=None, in_=table,
                    in_offset=bass.IndirectOffsetOnAxis(ap=stage_a[:, s, i:i + 1], axis=0),
                    bounds_check=bound, oob_is_err=False).then_inc(S[f"gathered{s}"], 16)

        def keep(j, s):
            pool_wait(pool, S[f"gathered{s}"], pg.ring_at("gathered", j, s), S["apart"])
            g.tensor_copy(result[:, bass.ds(j * 4, 4)], got[:, s, :]).then_inc(S["kept"], 1)
        skewed(pool, turns, [(0, ask), (1, keep)], ring=2)
        pool.wait_ge(S["kept"], pg.end("kept"))

    gather(m["src_i"], m["pos_tab"], m["src_row1"], NPAD - 1)
    gather(m["dst_i"], m["pos_tab"], m["dst_row"], NPAD - 1, prefill=m["zero_i"])

    pf = counts.phase(turns, {"index_set": 1, "scattered*": 64}, ring=2)

    def put(j, s):
        if not isinstance(j, int) or j >= 2:
            pool_wait(pool, S[f"scattered{s}"], pf.ring_at("scattered", j, s, back=1), S["apart"])
        g.tensor_copy(stage_a[:, s, :], free_i[:, bass.ds(j * 4, 4)])
        g.tensor_copy(stage_b[:, s, :], m["slot_id_i"][:, bass.ds(j * 4, 4)]).then_inc(S["index_set"], 1)
        pool_wait(pool, S["index_set"], pf.at("index_set", j), S["apart"])
        for i in range(4):
            pool.indirect_dma_start(
                out=m["free_tab"], in_=stage_b[:, s, i:i + 1], in_offset=None,
                out_offset=bass.IndirectOffsetOnAxis(ap=stage_a[:, s, i:i + 1], axis=0),
                bounds_check=SLOTS - 1, oob_is_err=False).then_inc(S[f"scattered{s}"], 16)
    skewed(pool, turns, [(0, put)], ring=2)
    for s in range(2):
        pool.wait_ge(S[f"scattered{s}"], pf.ring_end("scattered", s))

    rank_f, far_f = m["rank_f"], m["far_f"]
    def link(ins, n):
        ins.then_inc(S["pool_linked"], 1)
        pool.wait_ge(S["pool_linked"], n)
    link(g.tensor_copy(rank_f[:], m["src_row1"][:]), 1)
    link(g.tensor_scalar(far_f[:], rank_f[:], float(FILL), float(NONE), ALU.is_lt, ALU.mult), 2)
    link(g.tensor_scalar(rank_f[:], rank_f[:], float(-FILL), 0.0, ALU.add, ALU.max), 3)
    link(g.tensor_tensor(rank_f[:], rank_f[:], far_f[:], ALU.add), 4)
    link(g.tensor_copy(free_i[:], rank_f[:]), 5)
    gather(free_i, m["free_tab"], m["src_row"], SLOTS - 1, prefill=m["src_row1"])


def split_weights(nc, a, S, m):
    parts = [("w1", 1, H2, "L0_gnn_W1"), ("wf1", 2, H2, "L0_gnn_Wf1"), ("wf2", 2, H2, "L0_gnn_Wf2"),
             ("w2", 2, D, "L0_gnn_W2")]
    with nc.sbuf_tensor("w_in", [P, 4, 2, H2], F32) as w_in, nc.sbuf_tensor("b_rest", [P, H2], F32) as b_rest:
        with nc.Block() as block:
            @block.sync
            def _(sp):
                for n, (name, ks, width, key) in enumerate(parts):
                    sp.dma_start(w_in[:, n, 0:ks, 0:width], a[key].rearrange("(k p) n -> p k n", p=P)
                                 ).then_inc(S["weights_in"], 16)
                for name, key, width in (("b1", "L0_gnn_b1", H2), ("bf1", "L0_gnn_bf1", H2),
                                         ("bf2", "L0_gnn_bf2", H2), ("b2", "L0_gnn_b2", D)):
                    sp.dma_start(m[name][:], a[key].partition_broadcast(P)).then_inc(S["biases_in"], 16)
                sp.wait_ge(S["biases_in"], 64)

            @block.scalar
            def _(act):
                act.wait_ge(S["weights_in"], 64)
                for n, (name, ks, width, _) in enumerate(parts):
                    last = nc.scalar.activation(m[name + "_hi"][:, 0:ks, :], w_in[:, n, 0:ks, 0:width], ACT.Copy)
                last.then_inc(S["w_hi"], 1)
                act.wait_ge(S["biases_in"], 64)
                nc.scalar.activation(m["bf2_parts"][:], m["bf2"][:], ACT.Copy).then_inc(S["b_hi"], 1)

            @block.vector
            def _(dve):
                dve.wait_ge(S["weights_in"], 64)
                dve.wait_ge(S["w_hi"], 1)
                dve.wait_ge(S["biases_in"], 64)
                for r, s in enumerate((0.5, 0.5, 1.0, 1 / 6)):
                    nc.vector.tensor_scalar(m[f"bf2_{r}"][:], m["bf2"][:], s, None, ALU.mult)
                for n, (name, ks, width, _) in enumerate(parts):
                    nc.vector.tensor_tensor(m[name + "_lo"][:, 0:ks, :], w_in[:, n, 0:ks, 0:width],
                                            m[name + "_hi"][:, 0:ks, :].bitcast(F32), ALU.subtract)
                nc.vector.tensor_scalar(m["ones_r"][:], m["ident"][:], 0.0, 1.0, ALU.mult, ALU.add)
                dve.wait_ge(S["b_hi"], 1)
                nc.vector.tensor_tensor(b_rest[:], m["bf2"][:], m["bf2_parts"][:].bitcast(F32), ALU.subtract
                                        ).then_inc(S["b_split"], 1)
                dve.wait_ge(S["b_split"], 1)
                nc.vector.tensor_scalar(b_rest[:], b_rest[:], m["ident"][:, 1:2], None, ALU.mult
                                        ).then_inc(S["b_split"], 1)
                dve.wait_ge(S["b_split"], 2)
                nc.vector.scalar_tensor_tensor(m["bf2_parts"][:], m["bf2_parts"][:].bitcast(F32), m["ident"][:, 0:1],
                                               b_rest[:], ALU.mult, ALU.add)


def product(nc, out, hi, lo, w_hi, w_lo, ks, bias=None):
    n, last = 0, None
    for x, w in ((hi, w_hi), (hi, w_lo), (lo, w_hi)):
        for k in range(ks):
            last = nc.tensor.matmul(out, x(k), w[:, k, :], start=(n == 0), stop=(n == 3 * ks - 1 and not bias))
            n += 1
    if bias:
        last = nc.tensor.matmul(out, bias[0][:], bias[1][:], start=False, stop=True)
    return last


def local_pass(nc, a, S, counts, m):
    from contextlib import ExitStack
    ctx = ExitStack()

    def sb(name, shape, dt=F32):
        return ctx.enter_context(nc.sbuf_tensor(name, list(shape), dt))

    G, C = 5, 10
    Q = G * C
    blocks = TL // (2 * G)
    kind = ["first"] + ["mid", "end"] * 4 + ["last"]
    psum, ident = m["psum"], m["ident"]
    v = nc.vector
    split_weights(nc, a, S, m)
    with ctx:
        m["stage_a"] = sb("stage_a", [P, 2, 4], I32)
        m["stage_b"] = sb("stage_b", [P, 2, 4], I32)
        m["got"] = sb("got", [P, 2, 4], I32)
        m["rank_f"] = sb("rank_f", [P, TE])
        m["far_f"] = sb("far_f", [P, TE])
        x_in = sb("lx_in", [P, G, 2, XW])
        x_add = sb("lx_add", [P, G, 2, D])
        z = [sb(f"lz{i}", [P, G, 2, H2]) for i in range(4)]
        t = sb("lt", [P, G, 2, H2])
        xf = sb("lxf", [P, G, 2, H2])
        x1 = sb("lx1", [P, G, 2, D])
        rest = sb("lrest", [P, G, 2, H2])
        x_hi = sb("lx_hi", [P, 2, 2, H2], F32R)
        x_lo = sb("lx_lo", [P, 2, 2, H2], F32R)
        squares = sb("lsquares", [P, 2, H2])
        ss = sb("lss", [P, G, 2])
        root = sb("lroot", [P, G, 2])
        inv = sb("linv", [P, G, 2])
        inv2 = sb("linv2", [P, G, 2])
        stats = sb("lstats", [P, G, 2, 6])
        mv = sb("lmv", [P, G, 2, 2])

        source = {0: None, 9: xf}
        target, table = {0: z[0], 9: x1}, {0: m["z_tab"][0], 9: m["x1_tab"]}
        for r in range(4):
            source[2 * r + 1], target[2 * r + 1], table[2 * r + 1] = z[r], t, m["t_tab"][r]
            source[2 * r + 2] = t
            target[2 * r + 2] = z[r + 1] if r < 3 else xf
            table[2 * r + 2] = m["z_tab"][r + 1] if r < 3 else m["xf_tab"]

        def out_name(g, too):
            return f"stored_too{g}" if too else f"stored{g}"

        def store_class(c):
            return 1 if kind[c] == "mid" else 0

        normed = [1 if kind[q // G] in ("first", "mid") else 0 for q in range(Q)]
        rooted = [1 if kind[q // G] != "end" else 0 for q in range(Q)]
        one = [1] * Q
        rates = {
            "turned": one, "high": one, "low": one, "product": one, "taken": one,
            "rest_set": [[0, 0, 0, 0, 1, 0, 1, 0, 3, 1][q // G] for q in range(Q)],
            "rest_begun": [1 if q // G in (2, 8) else 0 for q in range(Q)],
            "chain": [2 if kind[q // G] == "last" else 0 for q in range(Q)],
            "squared": normed, "clamped": rooted, "rooted": rooted, "inverted": [5 * x for x in rooted],
            "done_act": normed, "done": [1 if kind[q // G] == "last" else 0 for q in range(Q)],
        }
        for g in range(G):
            rates[f"own_in{g}"] = [16 if q == g else 0 for q in range(Q)]
            rates[f"others_in{g}"] = [16 if q == 9 * G + g else 0 for q in range(Q)]
            for odd in range(2):
                rates[out_name(g, odd)] = [16 if q % G == g and store_class(q // G) == odd else 0 for q in range(Q)]
        ph = BlockPhase(counts, blocks, rates)

        def done(b, q):
            name = {"end": "taken", "last": "done"}.get(kind[q // G], "done_act")
            return S[name], ph.at(name, b, q)

        def before(b, q, n):
            if q >= n:
                return b, q - n
            return None if isinstance(b, int) and b == 0 else (b - 1, q - n + Q)

        with nc.Block() as block:
            @block.gpsimd
            def _(pool):
                edge_tables(nc, S, counts, m, pool)

            @block.sync
            def _(sp):
                def load(b, q):
                    g = q
                    if q >= G:
                        return
                    if not isinstance(b, int) or b > 0:
                        sp.wait_ge(S["taken"], ph.at("taken", b - 1, q))
                    sp.dma_start(x_in[:, g, :, :], m["x_tab"].rearrange("(t p) c -> p t c", p=P)[
                        :, bass.ds((b * G + g) * 2 + TE, 2), :]).then_inc(S[f"own_in{g}"], 16)

                def load_again(b, q):
                    c, g = q // G, q % G
                    if kind[c] != "last":
                        return
                    if not isinstance(b, int) or b > 0:
                        sp.wait_ge(S["rest_set"], ph.at("rest_set", b - 1, q))
                    sp.dma_start(x_add[:, g, :, :], m["x_tab"].rearrange("(t p) c -> p t c", p=P)[
                        :, bass.ds((b * G + g) * 2 + TE, 2), 0:D]).then_inc(S[f"others_in{g}"], 16)

                def store(b, q):
                    c, g = q // G, q % G
                    sp.wait_ge(*done(b, q))
                    sp.dma_start(table[c].rearrange("(t p) c -> p t c", p=P)[:, bass.ds((b * G + g) * 2 + TE, 2), :],
                                 target[c][:, g, :, :]).then_inc(S[out_name(g, store_class(c))], 16)
                skewed_blocks(sp, blocks, Q, [(0, load), (12, load_again), (24, store)])
                for g in range(G):
                    for odd in range(2):
                        sp.wait_ge(S[out_name(g, odd)], ph.end(out_name(g, odd)))

            @block.tensor
            def _(pe):
                def turn(b, q):
                    c, g = q // G, q % G
                    if c == 0:
                        pe.wait_ge(S[f"own_in{g}"], ph.at(f"own_in{g}", b, q))
                    else:
                        pe.wait_ge(*done(b, q - G))
                    prev = before(b, q, 2)
                    if prev:
                        pe.wait_ge(S["low"], ph.at("low", *prev))
                    src = x_in if c == 0 else source[c]
                    for k in range(1 if c == 0 else 2):
                        for i in range(2):
                            last = nc.tensor.transpose(psum[q % 2][:, k * H2 + i * P:k * H2 + (i + 1) * P],
                                                       src[:, g, i, k * P:(k + 1) * P], ident[:])
                    last.then_inc(S["turned"], 1)

                def multiply(b, q):
                    c = q // G
                    pe.wait_ge(S["high"], ph.at("high", b, q))
                    pe.wait_ge(S["low"], ph.at("low", b, q))
                    prev = before(b, q, 2)
                    if prev:
                        pe.wait_ge(S["taken"], ph.at("taken", *prev))
                    w, ks, width = {"first": ("w1", 1, H2), "mid": ("wf1", 2, H2), "end": ("wf2", 2, H2),
                                    "last": ("w2", 2, D)}[kind[c]]
                    for i in range(2):
                        last = product(nc, psum[2 + q % 2][:, i * width:(i + 1) * width],
                                       lambda k: x_hi[:, q % 2, k, i * P:(i + 1) * P],
                                       lambda k: x_lo[:, q % 2, k, i * P:(i + 1) * P],
                                       m[w + "_hi"], m[w + "_lo"], ks,
                                       (m["ones_r"], m["bf2_parts"]) if kind[c] == "end" else None)
                    last.then_inc(S["product"], 1)
                skewed_blocks(pe, blocks, Q, [(0, turn), (1, multiply)])

            @block.scalar
            def _(act):
                def high(b, q):
                    n = H2 if q // G == 0 else 2 * H2
                    act.wait_ge(S["turned"], ph.at("turned", b, q))
                    prev = before(b, q, 2)
                    if prev:
                        act.wait_ge(S["product"], ph.at("product", *prev))
                    nc.scalar.activation(x_hi[:, q % 2].rearrange("p k n -> p (k n)")[:, 0:n], psum[q % 2][:, 0:n],
                                         ACT.Copy).then_inc(S["high"], 1)

                def begin_rest(b, q):
                    c, g = q // G, q % G
                    if c not in (2, 8):
                        return
                    act.wait_ge(S["done_act"], ph.at("done_act", b, g))
                    if c == 8:
                        act.wait_ge(S["taken"], ph.at("taken", b, q - 2 * G))
                    elif not isinstance(b, int) or b > 0:
                        act.wait_ge(S["taken"], ph.at("taken", b - 1, 9 * G + g))
                    nc.scalar.activation(rest[:, g, :, :], z[0][:, g, :, :], ACT.Copy, scale=1.5 if c == 2 else -1 / 3
                                         ).then_inc(S["rest_begun"], 1)

                def scale(b, q):
                    if not normed[q]:
                        return
                    c, g = q // G, q % G
                    act.wait_ge(S["inverted"], ph.at("inverted", b, q))
                    for i in range(2):
                        last = nc.scalar.activation(target[c][:, g, i, :], target[c][:, g, i, :], ACT.Copy,
                                                    scale=inv[:, g, i:i + 1])
                    last.then_inc(S["done_act"], 1)

                def square(b, q):
                    if not normed[q]:
                        return
                    c, g = q // G, q % G
                    act.wait_ge(S["taken"], ph.at("taken", b, q))
                    for i in range(2):
                        last = nc.scalar.activation(squares[:, i, :], target[c][:, g, i, :], ACT.Square,
                                                    accum_out=ss[:, g, i:i + 1])
                    last.then_inc(S["squared"], 1)

                def take_root(b, q):
                    if not rooted[q]:
                        return
                    g = q % G
                    act.wait_ge(S["clamped"], ph.at("clamped", b, q))
                    nc.scalar.activation(root[:, g, :], ss[:, g, :], ACT.Sqrt).then_inc(S["rooted"], 1)
                skewed_blocks(act, blocks, Q, [(0, high), (1, begin_rest), (4, scale), (3, square), (3, take_root)])

            @block.vector
            def _(dve):
                def invert(b, q):
                    if not rooted[q]:
                        return
                    c, g = q // G, q % G
                    dve.wait_ge(S["rooted"], ph.at("rooted", b, q))
                    steps = [lambda: v.reciprocal(inv[:, g, :], root[:, g, :]),
                             lambda: v.tensor_tensor(inv2[:, g, :], inv[:, g, :], inv[:, g, :], ALU.mult),
                             lambda: v.tensor_tensor(inv2[:, g, :], inv2[:, g, :], ss[:, g, :], ALU.mult),
                             lambda: v.tensor_scalar(inv2[:, g, :], inv2[:, g, :], -0.5, 1.5, ALU.mult, ALU.add),
                             lambda: v.tensor_tensor(inv[:, g, :], inv[:, g, :], inv2[:, g, :], ALU.mult)]
                    for n, step in enumerate(steps):
                        if n:
                            dve.wait_ge(S["inverted"], ph.at("inverted", b, q, n))
                        step().then_inc(S["inverted"], 1)
                    if kind[c] == "last":
                        dve.wait_ge(S["inverted"], ph.at("inverted", b, q))
                        for i in range(2):
                            last = v.tensor_scalar(x1[:, g, i, :], x1[:, g, i, :], mv[:, g, i, 0:1], inv[:, g, i:i + 1],
                                                   ALU.subtract, ALU.mult)
                        last.then_inc(S["done"], 1)

                def low(b, q):
                    n = H2 if q // G == 0 else 2 * H2
                    dve.wait_ge(S["high"], ph.at("high", b, q))
                    v.tensor_tensor(x_lo[:, q % 2].rearrange("p k n -> p (k n)")[:, 0:n], psum[q % 2][:, 0:n],
                                    x_hi[:, q % 2].rearrange("p k n -> p (k n)")[:, 0:n].bitcast(F32),
                                    ALU.subtract).then_inc(S["low"], 1)

                def bias(name, width):
                    return m[name][:].unsqueeze(1).to_broadcast([P, 2, width])

                def add_rest(b, q):
                    c, g = q // G, q % G
                    if kind[c] == "end":
                        r = c // 2 - 1
                        if r in (1, 2):
                            v.scalar_tensor_tensor(rest[:, g, :, :], z[r][:, g, :, :], RK[r], z[0][:, g, :, :],
                                                   ALU.mult, ALU.add).then_inc(S["rest_set"], 1)
                        elif r == 3:
                            dve.wait_ge(S["rest_begun"], ph.at("rest_begun", b, q))
                            for n, s in enumerate((1 / 3, 2 / 3, 0.5)):
                                if n:
                                    dve.wait_ge(S["rest_set"], ph.at("rest_set", b, q, n))
                                v.scalar_tensor_tensor(rest[:, g, :, :], z[n + 1][:, g, :, :], s, rest[:, g, :, :],
                                                       ALU.mult, ALU.add).then_inc(S["rest_set"], 1)
                    elif kind[c] == "last":
                        dve.wait_ge(S[f"others_in{g}"], ph.at(f"others_in{g}", b, q))
                        v.tensor_tensor(rest[:, g, :, 0:D], x_add[:, g, :, :], bias("b2", D), ALU.add
                                        ).then_inc(S["rest_set"], 1)

                def take(b, q):
                    c, g = q // G, q % G
                    y = psum[2 + q % 2][:, 0:2 * H2].rearrange("p (i n) -> p i n", i=2)
                    out = target[c][:, g, :, :]
                    stored = [0, 2, 4, 6, 8, 9] if store_class(c) == 0 else [1, 3, 5, 7]
                    at = stored.index(c)
                    name = out_name(g, store_class(c))
                    if at > 0:
                        dve.wait_ge(S[name], ph.at(name, b, stored[at - 1] * G + g))
                    elif not isinstance(b, int) or b > 0:
                        dve.wait_ge(S[name], ph.at(name, b - 1, stored[-1] * G + g))
                    if kind[c] == "end":
                        b_scale = (0.5, 0.5, 1.0, 1 / 6)[c // 2 - 1]
                        if c == 2:
                            dve.wait_ge(S["rest_begun"], ph.at("rest_begun", b, q))
                        else:
                            dve.wait_ge(S["rest_set"], ph.at("rest_set", b, q))
                        dve.wait_ge(S["product"], ph.at("product", b, q))
                        v.scalar_tensor_tensor(out, y, b_scale, rest[:, g, :, :], ALU.mult, ALU.add
                                               ).then_inc(S["taken"], 1)
                    elif kind[c] == "last":
                        dve.wait_ge(S["rest_set"], ph.at("rest_set", b, q))
                        dve.wait_ge(S["product"], ph.at("product", b, q))
                        v.tensor_tensor(out, psum[2 + q % 2][:, 0:2 * D].rearrange("p (i n) -> p i n", i=2),
                                        rest[:, g, :, 0:D], ALU.add).then_inc(S["taken"], 1)
                        dve.wait_ge(S["taken"], ph.at("taken", b, q))
                        for i in range(2):
                            last = v.bn_stats(stats[:, g, i, :], out[:, i, :])
                        last.then_inc(S["chain"], 1)
                        pool_wait(dve, S["chain"], ph.at("chain", b, q, 1), S["apart"])
                        for i in range(2):
                            last = v.bn_aggr(mv[:, g, i, :], stats[:, g, i, :])
                        last.then_inc(S["chain"], 1)
                    else:
                        if c == 0:
                            v.tensor_copy(m["node_of"][:, bass.ds((b * G + g) * 2 + TE, 2)], x_in[:, g, :, D])
                        dve.wait_ge(S["product"], ph.at("product", b, q))
                        v.tensor_tensor(out, y, bias({"first": "b1", "mid": "bf1"}[kind[c]], H2), ALU.add
                                        ).then_inc(S["taken"], 1)

                def clamp(b, q):
                    c, g = q // G, q % G
                    if kind[c] == "last":
                        dve.wait_ge(S["chain"], ph.at("chain", b, q))
                        v.tensor_scalar(ss[:, g, :], mv[:, g, :, 1], LN_EPS, None, ALU.add
                                        ).then_inc(S["clamped"], 1)
                    elif normed[q]:
                        dve.wait_ge(S["squared"], ph.at("squared", b, q))
                        v.tensor_scalar(ss[:, g, :], ss[:, g, :], L2_EPS ** 2, None, ALU.max
                                        ).then_inc(S["clamped"], 1)
                skewed_blocks(dve, blocks, Q, [(2, add_rest), (1, low), (4, invert), (2, take), (3, clamp)])


def coupled_stages(nc, a, S, counts, m):
    from contextlib import ExitStack
    ctx = ExitStack()

    def sb(name, shape, dt=F32):
        t = ctx.enter_context(nc.sbuf_tensor(name, list(shape), dt))
        m[name] = t
        return t

    with ctx:
        sb("c_own", [P, 4, 2, H2])
        sb("c_rows", [P, 4, 2, H2])
        sb("c_sums", [P, 4, 2, P])
        for i in range(4):
            sb(f"c_z{i}", [P, 4, 2, H2])
        sb("y", [P, 4, 2, H2])
        sb("c_u", [P, 2, 2, H2])
        sb("c_rest", [P, 2, 2, H2])
        sb("c_hi", [P, 2, 2, H2], F32R)
        sb("c_lo", [P, 2, 2, H2], F32R)
        sb("c_squares", [P, 2, H2])
        sb("c_ss", [P, 4, 2])
        sb("c_inv", [P, 4, 2])
        sb("stats", [P, 4, 2, 6])
        sb("c_mv", [P, 4, 2, 2])
        sb("c_index", [P, 4, 4], I32)
        sb("c_scale", [P, TE])
        sb("c_neg_half", [P, 2])
        z = m["z_tab"]
        coupled_stage(nc, S, counts, m, "first", 0, m["x_tab"], z[0], [])
        for r in range(4):
            coupled_stage(nc, S, counts, m, "mid", r, z[r], m["t_tab"][r], [])
            res = [[z[0]], [z[1], z[0]], [z[2], z[0]], [z[1], z[2], z[3], z[0]]][r]
            coupled_stage(nc, S, counts, m, "end", r, m["t_tab"][r], (z[1:] + [m["xf_tab"]])[r], res)
        coupled_stage(nc, S, counts, m, "last", 0, m["xf_tab"], m["x1_tab"], [m["xo_tab"]])


def coupled_stage(nc, S, counts, m, kind, r, source, target, others):
    first, mid, end, final = (kind == k for k in ("first", "mid", "end", "last"))
    normed = first or mid
    rooted = normed or final
    pairs = TE // 2
    ks = 1 if first else 2
    win = D if first else H2
    wout = D if final else H2
    w = {"first": "w1", "mid": "wf1", "end": "wf2", "last": "w2"}[kind]
    v, psum, ident = nc.vector, m["psum"], m["ident"]
    own, rows, sums, y, u, rest = (m[n] for n in ("c_own", "c_rows", "c_sums", "y", "c_u", "c_rest"))
    x_hi, x_lo, ss, inv = (m[n] for n in ("c_hi", "c_lo", "c_ss", "c_inv"))
    index, scale_, dinv = m["c_index"], m["c_scale"], m["dinv"]
    zs = [m[f"c_z{i}"] for i in range(4)]
    n_rest = [1, 1, 1, 4][r] + 1 if end else 1 if final else 0
    own_in = "own_gathered" if first else "own_in"
    ph = counts.phase(pairs, {
        "index_set": 1, "gathered*": 32, own_in + "*": 32 if first else 16, "sums_in*": 16,
        "others_in*": 16 * len(others), "scaled": 2 if first else 0, "carried": 2, "summed": 2,
        "own_scaled": 1 if first else 0, "u_set": 1, "turned": 1, "high": 1, "low": 1,
        "product": 1, "taken": 1, "rest_set": n_rest, "squared": 1 if normed else 0,
        "chain": 2 if final else 0, "clamped": 1 if rooted else 0,
        "inverted": (2 if normed else 1) if rooted else 0, "done": 0 if end else 1, "stored*": 16,
        "stored_too*": 16 if first else 0})
    done = "taken" if end else "done"
    ready = 6 if rooted else 4

    def past(j, n):
        return not isinstance(j, int) or j >= n

    def tiles(table, j, width):
        return table.rearrange("(t p) c -> p t c", p=P)[:, bass.ds(j * 2, 2), 0:width]

    def row_width(t):
        return t[:, :, :, 0:XW] if first else t

    with nc.Block() as block:
        @block.sync
        def _(sp):
            def load(j, s):
                if past(j, 4):
                    sp.wait_ge(S["summed"], ph.at("summed", j - 4))
                sp.dma_start(sums[:, s, :, :], m["sum_tab"][bass.ds(j * 2, 2), :, :].rearrange("t p f -> p t f")
                             ).then_inc(S[f"sums_in{s}"], 16)
                if not first:
                    if past(j, 4):
                        sp.wait_ge(S["u_set"], ph.at("u_set", j - 4))
                    sp.dma_start(own[:, s, :, :], tiles(source, j, H2)).then_inc(S[f"own_in{s}"], 16)
                else:
                    pass

            def load_others(j, s):
                if past(j, 4):
                    sp.wait_ge(S["taken"], ph.at("taken", j - 4))
                for n, table in enumerate(others):
                    width = D if final else H2
                    sp.dma_start(zs[n][:, s, :, 0:width], tiles(table, j, width)
                                 ).then_inc(S[f"others_in{s}"], 16)

            def store_x(j, s):
                sp.wait_ge(S[f"{own_in}{s}"], ph.ring_at(own_in, j, s))
                sp.dma_start(tiles(m["xo_tab"], j, D), own[:, s, :, 0:D]).then_inc(S[f"stored_too{s}"], 16)

            steps = [(0, load)]
            if others:
                steps.append((3, load_others))
            if first:
                steps.append((3, store_x))
            skewed(sp, pairs, steps)
            if first:
                for s in range(4):
                    sp.wait_ge(S[f"stored_too{s}"], ph.ring_end("stored_too", s))

        @block.gpsimd
        def _(pool):
            def gather(j, s):
                if past(j, 4):
                    pool_wait(pool, S["summed"], ph.at("summed", j - 4), S["apart"])
                    if first:
                        pool_wait(pool, S["u_set"], ph.at("u_set", j - 4), S["apart"])
                        pool_wait(pool, S[f"stored_too{s}"], ph.ring_at("stored_too", j, s, back=1), S["apart"])
                which = m["src_row1"] if first else m["src_row"]
                if first:
                    nc.gpsimd.tensor_copy(index[:, s, 2:4], m["own_row"][:, bass.ds(j * 2, 2)])
                nc.gpsimd.tensor_copy(index[:, s, 0:2], which[:, bass.ds(j * 2, 2)]).then_inc(S["index_set"], 1)
                pool_wait(pool, S["index_set"], ph.at("index_set", j), S["apart"])
                for i in range(2):
                    pool.indirect_dma_start(
                        out=rows[:, s, i, 0:XW] if first else rows[:, s, i, :], out_offset=None, in_=source,
                        in_offset=bass.IndirectOffsetOnAxis(ap=index[:, s, i:i + 1], axis=0)
                    ).then_inc(S[f"gathered{s}"], 16)
                if first:
                    for i in range(2):
                        pool.indirect_dma_start(
                            out=own[:, s, i, 0:XW], out_offset=None, in_=source,
                            in_offset=bass.IndirectOffsetOnAxis(ap=index[:, s, 2 + i:3 + i], axis=0)
                        ).then_inc(S[f"{own_in}{s}"], 16)

            def invert(j, s):
                if final:
                    pool_wait(pool, S["chain"], ph.at("chain", j), S["apart"])
                    nc.gpsimd.tensor_scalar(ss[:, s, :], m["c_mv"][:, s, :, 1], LN_EPS, None, ALU.add
                                            ).then_inc(S["clamped"], 1)
                else:
                    pool_wait(pool, S["squared"], ph.at("squared", j), S["apart"])
                    nc.gpsimd.tensor_scalar(ss[:, s, :], ss[:, s, :], L2_EPS ** 2, None, ALU.max
                                            ).then_inc(S["clamped"], 1)
                pool_wait(pool, S["clamped"], ph.at("clamped", j), S["apart"])
                nc.gpsimd.tensor_tensor(inv[:, s, :], ss[:, s, :], m["c_neg_half"][:], ALU.pow
                                        ).then_inc(S["inverted"], 1)
                if normed:
                    pool_wait(pool, S["inverted"], ph.at("inverted", j, 1), S["apart"])
                    nc.gpsimd.tensor_tensor(inv[:, s, :], inv[:, s, :], dinv[:, bass.ds(j * 2, 2)], ALU.mult
                                            ).then_inc(S["inverted"], 1)
            if first:
                nc.gpsimd.memset(m["c_neg_half"][:], -0.5).then_inc(S["c_constants"], 1)
                pool.wait_ge(S["c_constants"], 1)
            skewed(pool, pairs, [(0, gather)] + ([(8, invert)] if rooted else []))

        @block.tensor
        def _(pe):
            def add_up(i):
                def step(j, s):
                    pe.wait_ge(S["carried"], ph.at("carried", j, i + 1))
                    if i == 0:
                        pe.wait_ge(S[f"sums_in{s}"], ph.ring_at("sums_in", j, s))
                        if past(j, 2):
                            pe.wait_ge(S["u_set"], ph.at("u_set", j - 2))
                    nc.tensor.matmul(psum[s % 2][:, i * win:(i + 1) * win], sums[:, s, i, :], rows[:, s, i, 0:win],
                                     start=True, stop=True).then_inc(S["summed"], 1)
                return step

            def turn(j, s):
                pe.wait_ge(S["u_set"], ph.at("u_set", j))
                if past(j, 2):
                    pe.wait_ge(S["low"], ph.at("low", j - 2))
                for k in range(ks):
                    for i in range(2):
                        last = nc.tensor.transpose(psum[2 + s % 2][:, k * H2 + i * P:k * H2 + (i + 1) * P],
                                                   u[:, s % 2, i, k * P:(k + 1) * P], ident[:])
                last.then_inc(S["turned"], 1)

            def multiply(j, s):
                pe.wait_ge(S["low"], ph.at("low", j))
                if past(j, 2):
                    pe.wait_ge(S["taken"], ph.at("taken", j - 2))
                for i in range(2):
                    last = product(nc, psum[4 + s % 2][:, i * wout:(i + 1) * wout],
                                   lambda k: x_hi[:, s % 2, k, i * P:(i + 1) * P],
                                   lambda k: x_lo[:, s % 2, k, i * P:(i + 1) * P], m[w + "_hi"], m[w + "_lo"], ks)
                last.then_inc(S["product"], 1)
            skewed(pe, pairs, [(0, add_up(0)), (2, turn), (0, add_up(1)), (3, multiply)])

        @block.scalar
        def _(act):
            n = ks * H2

            def high(j, s):
                act.wait_ge(S["turned"], ph.at("turned", j))
                if past(j, 2):
                    act.wait_ge(S["product"], ph.at("product", j - 2))
                nc.scalar.activation(x_hi[:, s % 2].rearrange("p k n -> p (k n)")[:, 0:n], psum[2 + s % 2][:, 0:n],
                                     ACT.Copy).then_inc(S["high"], 1)

            def scale(j, s):
                act.wait_ge(S["inverted"], ph.at("inverted", j))
                for i in range(2):
                    last = nc.scalar.activation(y[:, s, i, :], y[:, s, i, :], ACT.Copy, scale=inv[:, s, i:i + 1])
                last.then_inc(S["done"], 1)

            def square(j, s):
                act.wait_ge(S["taken"], ph.at("taken", j))
                if past(j, 1):
                    act.wait_ge(S["squared"], ph.at("squared", j - 1))
                for i in range(2):
                    last = nc.scalar.activation(m["c_squares"][:, i, :], y[:, s, i, :], ACT.Square,
                                                accum_out=ss[:, s, i:i + 1])
                last.then_inc(S["squared"], 1)
            def store(j, s):
                act.wait_ge(S[done], ph.at(done, j))
                act.dma_start(tiles(target, j, wout), y[:, s, :, 0:wout]).then_inc(S[f"stored{s}"], 16)
            steps = [(2, high)]
            if normed:
                steps.append((ready, scale))
            steps.append((ready, store))
            if normed:
                steps.append((4, square))
            skewed(act, pairs, steps)
            for s in range(4):
                act.wait_ge(S[f"stored{s}"], ph.ring_end("stored", s))

        @block.vector
        def _(dve):
            if end:
                v.scalar_tensor_tensor(scale_[:], dinv[:], (0.5, 0.5, 1.0, 1 / 6)[r], dinv[:], ALU.mult, ALU.mult
                                       ).then_inc(S["c_scale_set"], 1)
                dve.wait_ge(S["c_scale_set"], r + 1)

            def carry_on(i):
                p0 = (0, 96)[i]

                def step(j, s):
                    if i == 0:
                        dve.wait_ge(S[f"gathered{s}"], ph.ring_at("gathered", j, s))
                        if first:
                            for k in range(2):
                                v.tensor_scalar(rows[:, s, k, 0:D], rows[:, s, k, 0:D], rows[:, s, k, D + 1:D + 2],
                                                None, ALU.mult).then_inc(S["scaled"], 1)
                    if first:
                        dve.wait_ge(S["scaled"], ph.at("scaled", j, i + 1))
                    if i == 0 and isinstance(j, int) and j == 0:
                        dve.sem_inc(S["carried"], 1)
                        return
                    if i == 0:
                        dve.wait_ge(S["summed"], ph.at("summed", j - 1))
                        before = psum[(s + 1) % 2][p0:p0 + 32, win:2 * win]
                    else:
                        dve.wait_ge(S["summed"], ph.at("summed", j, 1))
                        before = psum[s % 2][p0:p0 + 32, 0:win]
                    v.scalar_tensor_tensor(rows[p0:p0 + 32, s, i, 0:win], before,
                                           m["carry"][p0:p0 + 32, bass.ds(j * 2 + i, 1)],
                                           rows[p0:p0 + 32, s, i, 0:win], ALU.mult, ALU.add
                                           ).then_inc(S["carried"], 1)
                return step

            def add_own(j, s):
                dve.wait_ge(S["summed"], ph.at("summed", j))
                dve.wait_ge(S[f"{own_in}{s}"], ph.ring_at(own_in, j, s))
                if past(j, 2):
                    dve.wait_ge(S["turned"], ph.at("turned", j - 2))
                if first:
                    v.tensor_copy(dinv[:, bass.ds(j * 2, 2)], own[:, s, :, D + 1])
                    v.tensor_copy(m["node_of"][:, bass.ds(j * 2, 2)], own[:, s, :, D])
                    for i in range(2):
                        last = v.tensor_scalar(u[:, s % 2, i, 0:D], own[:, s, i, 0:D], own[:, s, i, D + 1:D + 2],
                                               None, ALU.mult)
                    last.then_inc(S["own_scaled"], 1)
                    dve.wait_ge(S["own_scaled"], ph.at("own_scaled", j))
                for i in range(2):
                    last = v.scalar_tensor_tensor(
                        u[:, s % 2, i, 0:win], psum[s % 2][:, i * win:(i + 1) * win],
                        m["lead"][:, bass.ds(j * 2 + i, 1)],
                        u[:, s % 2, i, 0:win] if first else own[:, s, i, :], ALU.mult, ALU.add)
                last.then_inc(S["u_set"], 1)

            def low(j, s):
                n = ks * H2
                dve.wait_ge(S["high"], ph.at("high", j))
                v.tensor_tensor(x_lo[:, s % 2].rearrange("p k n -> p (k n)")[:, 0:n], psum[2 + s % 2][:, 0:n],
                                x_hi[:, s % 2].rearrange("p k n -> p (k n)")[:, 0:n].bitcast(F32),
                                ALU.subtract).then_inc(S["low"], 1)

            def add_rest(j, s):
                dve.wait_ge(S[f"others_in{s}"], ph.ring_at("others_in", j, s))
                count = [0]

                def rest_step(ins):
                    count[0] += 1
                    ins.then_inc(S["rest_set"], 1)
                pr = rest[:, s % 2, :, :]
                if final:
                    rest_step(v.tensor_tensor(pr[:, :, 0:D], zs[0][:, s, :, 0:D],
                                              m["b2"][:].unsqueeze(1).to_broadcast([P, 2, D]), ALU.add))
                elif r == 0:
                    rest_step(v.tensor_scalar(pr, zs[0][:, s, :, :], 1.5, None, ALU.mult))
                elif r < 3:
                    rest_step(v.scalar_tensor_tensor(pr, zs[0][:, s, :, :], RK[r], zs[1][:, s, :, :], ALU.mult, ALU.add))
                else:
                    rest_step(v.tensor_scalar(pr, zs[3][:, s, :, :], -1 / 3, None, ALU.mult))
                    for n, c in enumerate((1 / 3, 2 / 3, 0.5)):
                        dve.wait_ge(S["rest_set"], ph.at("rest_set", j, count[0]))
                        rest_step(v.scalar_tensor_tensor(pr, zs[n][:, s, :, :], c, pr, ALU.mult, ALU.add))
                if end:
                    dve.wait_ge(S["rest_set"], ph.at("rest_set", j, count[0]))
                    for i in range(2):
                        last = v.scalar_tensor_tensor(pr[:, i, :], m[f"bf2_{r}"][:], dinv[:, bass.ds(j * 2 + i, 1)],
                                                      pr[:, i, :], ALU.mult, ALU.add)
                    last.then_inc(S["rest_set"], 1)

            def take(j, s):
                bank, pr = psum[4 + s % 2], rest[:, s % 2, :, :]
                if past(j, 4):
                    dve.wait_ge(S[f"stored{s}"], ph.ring_at("stored", j, s, back=1))
                if normed:
                    dve.wait_ge(S["product"], ph.at("product", j))
                    for i in range(2):
                        last = v.scalar_tensor_tensor(y[:, s, i, :], bank[:, i * H2:(i + 1) * H2],
                                                      dinv[:, bass.ds(j * 2 + i, 1)], m[{"first": "b1", "mid": "bf1"}[kind]][:],
                                                      ALU.mult, ALU.add)
                    last.then_inc(S["taken"], 1)
                    return
                dve.wait_ge(S["rest_set"], ph.at("rest_set", j))
                dve.wait_ge(S["product"], ph.at("product", j))
                by = scale_ if end else dinv
                for i in range(2):
                    last = v.scalar_tensor_tensor(y[:, s, i, 0:wout], bank[:, i * wout:(i + 1) * wout],
                                                  by[:, bass.ds(j * 2 + i, 1)], pr[:, i, 0:wout], ALU.mult, ALU.add)
                last.then_inc(S["taken"], 1)
                if final:
                    dve.wait_ge(S["taken"], ph.at("taken", j))
                    for i in range(2):
                        last = v.bn_stats(m["stats"][:, s, i, :], y[:, s, i, 0:D])
                    last.then_inc(S["chain"], 1)
                    pool_wait(dve, S["chain"], ph.at("chain", j, 1), S["apart"])
                    for i in range(2):
                        last = v.bn_aggr(m["c_mv"][:, s, i, :], m["stats"][:, s, i, :])
                    last.then_inc(S["chain"], 1)

            def normalise(j, s):
                dve.wait_ge(S["inverted"], ph.at("inverted", j))
                for i in range(2):
                    last = v.tensor_scalar(y[:, s, i, 0:D], y[:, s, i, 0:D], m["c_mv"][:, s, i, 0:1],
                                           inv[:, s, i:i + 1], ALU.subtract, ALU.mult)
                last.then_inc(S["done"], 1)
            steps = [(0, carry_on(0)), (1, add_own), (3, low), (0, carry_on(1)), (4, take)]
            if not normed:
                steps.insert(1, (4, add_rest))
            if final:
                steps.append((ready, normalise))
            skewed(dve, pairs, steps)


def attention(nc, a, S, counts, m):
    from contextlib import ExitStack
    ctx = ExitStack()

    def sb(name, shape, dt=F32):
        t = ctx.enter_context(nc.sbuf_tensor(name, list(shape), dt))
        m[name] = t
        return t

    with ctx:
        sb("alpha", [P, TE, HEADS])
        sb("w_kvq", [P, 3 * D])
        sb("w_edge", [ED + 1, 3 * D])
        sb("w_skip", [P, D])
        sb("w_up", [P, D])
        sb("w_down", [P, D])
        sb("b_skip", [P, 1])
        sb("b_up", [P, 1])
        sb("b_down", [P, 1])
        sb("neg_half", [P, 2])
        scores(nc, a, S, counts, m)
        with nc.sbuf_tensor("run_max", [P, SLOTS // 32], F32) as run_max:
            run_maxima(nc, a, S, m, run_max)
        weighted_sums(nc, S, counts, m)
        finish(nc, S, counts, m, TE // 2, 0, True)
        finish(nc, S, counts, m, TL // 2, TE, False)


def scores(nc, a, S, counts, m):
    from contextlib import ExitStack
    ctx = ExitStack()

    def sb(name, shape, dt=F32):
        return ctx.enter_context(nc.sbuf_tensor(name, list(shape), dt))

    pairs = TE // 2
    v, psum, ident = nc.vector, m["psum"], m["ident"]
    ph = counts.phase(pairs, {"index_set": 1, "gathered*": 64, "own_in*": 16, "turned": 1, "copied": 1,
                              "product": 1, "query": 1, "values": 1, "weighed": 1, "alpha": 1,
                              "alpha_turned": 1, "line": 1, "stored*": 16, "stored_too*": 16})

    def past(j, n):
        return not isinstance(j, int) or j >= n

    with ctx:
        rows = sb("a_rows", [P, 4, 4, D])
        index = sb("a_idx", [P, 4, 4], I32)
        edge = sb("a_edge", [ED + 1, 4, 2 * P])
        xt = sb("a_xt", [P, 2, 4 * P])
        query = sb("a_q", [P, 2, 2, D])
        values = sb("a_v", [P, 4, 2, D])
        weighed = sb("a_w", [P, 2, 2, D])
        al = sb("a_al", [P, 4, 2, HEADS])
        line = sb("a_ln", [HEADS, 4, 2, P])
        with nc.Block() as block:
            @block.sync
            def _(sp):
                for n, key in enumerate(("Wk", "Wv", "Wq")):
                    sp.dma_start(m["w_kvq"][:, n * D:(n + 1) * D], a["L1_gnn_" + key]).then_inc(S["a_weights"], 16)
                for n in range(2):
                    sp.dma_start(m["w_edge"][0:ED, n * D:(n + 1) * D], a["L1_gnn_We"]).then_inc(S["a_weights"], 16)
                for n, key in enumerate(("bk", "bv", "bq")):
                    sp.dma_start(m["w_edge"][ED:ED + 1, n * D:(n + 1) * D], a["L1_gnn_" + key].unsqueeze(0)
                                 ).then_inc(S["a_weights"], 16)
                for name, key in (("w_skip", "Wskip"), ("w_up", "W1"), ("w_down", "W2")):
                    sp.dma_start(m[name][:], a["L1_gnn_" + key]).then_inc(S["a_weights"], 16)
                for name, key in (("b_skip", "bskip"), ("b_up", "b1"), ("b_down", "b2")):
                    sp.dma_start(m[name][:], a["L1_gnn_" + key].unsqueeze(1)).then_inc(S["a_weights"], 16)

                def load(j, s):
                    if past(j, 4):
                        sp.wait_ge(S["product"], ph.at("product", j - 4))
                    sp.dma_start(edge[:, s, :], a["edge_attr"][:, bass.ds(j * (2 * P), 2 * P)]
                                 ).then_inc(S[f"own_in{s}"], 16)

                def store(j, s):
                    sp.wait_ge(S["values"], ph.at("values", j))
                    sp.dma_start(m["v_tab"].rearrange("(t p) c -> p t c", p=P)[:, bass.ds(j * 2, 2), :],
                                 values[:, s, :, :]).then_inc(S[f"stored{s}"], 16)

                def store_line(j, s):
                    sp.wait_ge(S["line"], ph.at("line", j))
                    sp.dma_start(m["alpha_line"][:, bass.ds(j * (2 * P), 2 * P)],
                                 line[:, s, :, :].rearrange("h i p -> h (i p)")).then_inc(S[f"stored_too{s}"], 16)
                skewed(sp, pairs, [(0, load), (5, store), (7, store_line)])
                for s in range(4):
                    sp.wait_ge(S[f"stored{s}"], ph.ring_end("stored", s))
                    sp.wait_ge(S[f"stored_too{s}"], ph.ring_end("stored_too", s))
                sp.wait_ge(S["a_weights"], 224)

            @block.gpsimd
            def _(pool):
                nc.gpsimd.memset(m["neg_half"][:], -0.5).then_inc(S["a_constants"], 1)

                def gather(j, s):
                    if past(j, 4):
                        pool_wait(pool, S["turned"], ph.at("turned", j - 4), S["apart"])
                        pool_wait(pool, S[f"gathered{s}"], ph.ring_at("gathered", j, s, back=1), S["apart"])
                    nc.gpsimd.tensor_copy(index[:, s, 0:2], m["src_row"][:, bass.ds(j * 2, 2)])
                    nc.gpsimd.tensor_copy(index[:, s, 2:4], m["dst_row"][:, bass.ds(j * 2, 2)]).then_inc(S["index_set"], 1)
                    pool_wait(pool, S["index_set"], ph.at("index_set", j), S["apart"])
                    for i in range(4):
                        pool.indirect_dma_start(
                            out=rows[:, s, i, :], out_offset=None, in_=m["x1_tab"],
                            in_offset=bass.IndirectOffsetOnAxis(ap=index[:, s, i:i + 1], axis=0)
                        ).then_inc(S[f"gathered{s}"], 16)
                skewed(pool, pairs, [(0, gather)])

            @block.tensor
            def _(pe):
                pe.wait_ge(S["a_weights"], 224)
                pe.wait_ge(S["a_zeros"], 1)

                def turn(j, s):
                    pe.wait_ge(S[f"gathered{s}"], ph.ring_at("gathered", j, s))
                    if past(j, 2):
                        pe.wait_ge(S["copied"], ph.at("copied", j - 2))
                    for i in range(4):
                        last = nc.tensor.transpose(psum[s % 2][:, i * P:(i + 1) * P], rows[:, s, i, :], ident[:])
                    last.then_inc(S["turned"], 1)

                def multiply(j, s):
                    pe.wait_ge(S["copied"], ph.at("copied", j))
                    pe.wait_ge(S[f"own_in{s}"], ph.ring_at("own_in", j, s))
                    if past(j, 2):
                        pe.wait_ge(S["values"], ph.at("values", j - 2))
                        pe.wait_ge(S["weighed"], ph.at("weighed", j - 2))
                    for i in range(2):
                        bank = psum[2 + 2 * (s % 2) + i]
                        nc.tensor.matmul(bank[:, 0:3 * D], edge[:, s, i * P:(i + 1) * P], m["w_edge"][:],
                                         start=True, stop=False)
                        nc.tensor.matmul(bank[:, 0:2 * D], xt[:, s % 2, i * P:(i + 1) * P], m["w_kvq"][:, 0:2 * D],
                                         start=False, stop=False)
                        last = nc.tensor.matmul(bank[:, 2 * D:3 * D], xt[:, s % 2, (2 + i) * P:(3 + i) * P],
                                                m["w_kvq"][:, 2 * D:3 * D], start=False, stop=True)
                    last.then_inc(S["product"], 1)

                def turn_alpha(j, s):
                    pe.wait_ge(S["alpha"], ph.at("alpha", j))
                    if past(j, 2):
                        pe.wait_ge(S["line"], ph.at("line", j - 2))
                    for i in range(2):
                        last = nc.tensor.transpose(psum[6 + s % 2][0:HEADS, i * P:(i + 1) * P], al[:, s, i, :], ident[:])
                    last.then_inc(S["alpha_turned"], 1)
                skewed(pe, pairs, [(0, turn), (1, multiply), (2, turn_alpha)])

            @block.scalar
            def _(act):
                def copy(j, s):
                    act.wait_ge(S["turned"], ph.at("turned", j))
                    if past(j, 2):
                        act.wait_ge(S["product"], ph.at("product", j - 2))
                    nc.scalar.activation(xt[:, s % 2, :], psum[s % 2][:], ACT.Copy).then_inc(S["copied"], 1)

                def take(j, s):
                    act.wait_ge(S["product"], ph.at("product", j))
                    if past(j, 4):
                        act.wait_ge(S[f"stored{s}"], ph.ring_at("stored", j, s, back=1))
                    for i in range(2):
                        last = nc.scalar.activation(values[:, s, i, :], psum[2 + 2 * (s % 2) + i][:, D:2 * D], ACT.Copy)
                    last.then_inc(S["values"], 1)
                    if past(j, 2):
                        act.wait_ge(S["weighed"], ph.at("weighed", j - 2))
                    for i in range(2):
                        last = nc.scalar.activation(query[:, s % 2, i, :], psum[2 + 2 * (s % 2) + i][:, 2 * D:3 * D],
                                                    ACT.Copy, scale=HC ** -0.5)
                    last.then_inc(S["query"], 1)
                skewed(act, pairs, [(0, copy), (1, take)])

            @block.vector
            def _(dve):
                v.memset(m["w_edge"][0:ED, 2 * D:3 * D], 0.0).then_inc(S["a_zeros"], 1)

                def weigh(j, s):
                    dve.wait_ge(S["query"], ph.at("query", j))
                    if past(j, 4):
                        dve.wait_ge(S["alpha_turned"], ph.at("alpha_turned", j - 4))
                    for i in range(2):
                        last = v.tensor_tensor(weighed[:, s % 2, i, :], psum[2 + 2 * (s % 2) + i][:, 0:D],
                                               query[:, s % 2, i, :], ALU.mult)
                    last.then_inc(S["weighed"], 1)
                    dve.wait_ge(S["weighed"], ph.at("weighed", j))
                    v.tensor_reduce(al[:, s, :, :].rearrange("p i h -> p (i h)"),
                                    weighed[:, s % 2, :, :].rearrange("p i (h c) -> p (i h) c", c=HC),
                                    AX.X, ALU.add).then_inc(S["alpha"], 1)

                def keep(j, s):
                    dve.wait_ge(S["alpha"], ph.at("alpha", j))
                    v.tensor_copy(m["alpha"][:, bass.ds(j * 2, 2), :], al[:, s, :, :])
                    dve.wait_ge(S["alpha_turned"], ph.at("alpha_turned", j))
                    if past(j, 4):
                        dve.wait_ge(S[f"stored_too{s}"], ph.ring_at("stored_too", j, s, back=1))
                    v.tensor_copy(line[:, s, 0, :], psum[6 + s % 2][0:HEADS, 0:P])
                    v.tensor_copy(line[:, s, 1, :], psum[6 + s % 2][0:HEADS, 2 * P - 1:P - 1:-1]
                                  ).then_inc(S["line"], 1)
                skewed(dve, pairs, [(1, weigh), (3, keep)])


def run_maxima(nc, a, S, m, run_max):
    from contextlib import ExitStack
    ctx = ExitStack()

    def sb(name, shape, dt=F32):
        return ctx.enter_context(nc.sbuf_tensor(name, list(shape), dt))

    w = SLOTS // 32
    v, psum, ident = nc.vector, m["psum"], m["ident"]
    with ctx:
        ids_i = sb("r_ids_i", [P, 3, w], I32)
        ids = sb("r_ids", [P, 3, w])
        starts = sb("r_starts", [P, w])
        ends = sb("r_ends", [P, w])
        al = sb("r_al", [P, w])
        up_to = sb("r_up_to", [P, w])
        pair = sb("r_pair", [P, 2])
        row = sb("r_row", [2, P])
        row0 = sb("r_row0", [1, 3, P + 1])
        side = sb("r_side", [P, 2])
        with nc.Block() as block:
            @block.sync
            def _(sp):
                sp.dma_start(al[:], m["alpha_line"].rearrange("h (b w) -> (h b) w", w=w)).then_inc(S["r_in"], 16)
                for h in range(HEADS):
                    for n in range(3):
                        sp.dma_start(ids_i[32 * h:32 * h + 32, n, :],
                                     a["dst_line"][n:n + SLOTS].rearrange("(b w) -> b w", w=w)).then_inc(S["r_in"], 16)
                for d in range(2):
                    sp.wait_ge(S["r_row"], d + 1)
                    for n in range(2):
                        sp.dma_start(row0[0:1, n, 0:P], row[n:n + 1, :]).then_inc(S["r_row_in"], 16)
                sp.wait_ge(S["r_done"], 1)
                sp.dma_start(m["max_line"].rearrange("h (b w) -> (h b) w", w=w), run_max[:]).then_inc(S["r_out"], 16)
                sp.wait_ge(S["r_out"], 16)

            @block.tensor
            def _(pe):
                for d in range(2):
                    pe.wait_ge(S["r_pair"], d + 1)
                    nc.tensor.transpose(psum[0][0:2, 0:P], pair[:], ident[:]).then_inc(S["r_turned"], 1)
                    pe.wait_ge(S["r_side"], d + 1)
                    nc.tensor.transpose(psum[1][:, 0:1], row0[0:1, 2, 0:P], ident[0:1, 0:1]).then_inc(S["r_back"], 1)

            @block.vector
            def _(dve):
                n = [0]

                def link(ins):
                    n[0] += 1
                    ins.then_inc(S["r_linked"], 1)
                    dve.wait_ge(S["r_linked"], n[0])
                dve.wait_ge(S["r_in"], 16 * 13)
                link(v.tensor_copy(ids[:], ids_i[:]))
                link(v.tensor_tensor(starts[:], ids[:, 0, :], ids[:, 1, :], ALU.not_equal))
                link(v.tensor_tensor(ends[:], ids[:, 1, :], ids[:, 2, :], ALU.not_equal))
                link(v.tensor_scalar(starts[:], starts[:], NEG, None, ALU.mult))
                link(v.tensor_scalar(ends[:], ends[:], NEG, None, ALU.mult))
                for d in range(2):
                    def way(ap):
                        return ap[:, ::-1] if d else ap[:, :]
                    gate, values, result = ((starts, al, up_to), (ends, up_to, run_max))[d]
                    link(v.tensor_tensor_scan(way(result[:]), way(gate[:]), way(values[:]), 0.0, ALU.add, ALU.max))
                    at = 0 if d else w - 1
                    link(v.tensor_copy(pair[:, 0:1], result[:, at:at + 1]))
                    v.tensor_reduce(pair[:, 1:2], gate[:], AX.X, ALU.min).then_inc(S["r_pair"], 1)
                    dve.wait_ge(S["r_turned"], d + 1)
                    v.tensor_copy(row[:], psum[0][0:2, 0:P]).then_inc(S["r_row"], 1)
                    dve.wait_ge(S["r_row_in"], 32 * (d + 1))
                    block_max, block_gate = row0[0:1, 0, 0:P], row0[0:1, 1, 0:P]
                    out = row0[0:1, 2, 1:P + 1]
                    if d:
                        link(v.tensor_tensor_scan(row0[0:1, 2, 1:P + 1][:, ::-1], block_gate[:, ::-1],
                                                  block_max[:, ::-1], 0.0, ALU.add, ALU.max))
                        link(v.tensor_copy(row0[0:1, 0, 0:P - 1], row0[0:1, 2, 2:P + 1]))
                        link(v.tensor_copy(row0[0:1, 2, 0:P - 1], row0[0:1, 0, 0:P - 1]))
                        v.memset(row0[0:1, 2, P - 1:P], 0.0).then_inc(S["r_side"], 1)
                    else:
                        link(v.tensor_tensor_scan(out, block_gate, block_max, 0.0, ALU.add, ALU.max))
                        v.memset(row0[0:1, 2, 0:1], 0.0).then_inc(S["r_side"], 1)
                    dve.wait_ge(S["r_back"], d + 1)
                    link(v.tensor_copy(side[:, d:d + 1], psum[1][:, 0:1]))
                    last = v.tensor_tensor_scan(way(result[:]), way(gate[:]), way(values[:]), side[:, d:d + 1],
                                                ALU.add, ALU.max)
                    if d:
                        last.then_inc(S["r_done"], 1)
                    else:
                        link(last)


def weighted_sums(nc, S, counts, m):
    from contextlib import ExitStack
    ctx = ExitStack()

    def sb(name, shape, dt=F32):
        return ctx.enter_context(nc.sbuf_tensor(name, list(shape), dt))

    pairs = TE // 2
    wide = D + HEADS
    v, psum, ident = nc.vector, m["psum"], m["ident"]
    ph = counts.phase(pairs, {"others_in*": 16, "own_in*": 16, "sums_in*": 16, "ordered": 1, "turned": 1,
                              "less": 1, "exp": 1, "weighed": 1, "carried": 2, "summed": 2,
                              "den": 3, "done": 1, "stored*": 16})

    def past(j, n):
        return not isinstance(j, int) or j >= n

    with ctx:
        max_in = sb("w_max", [HEADS, 4, 2, P])
        ordered = sb("w_ord", [HEADS, 4, 2, P])
        v_in = sb("w_v", [P, 4, 2, D])
        sums = sb("w_sums", [P, 4, 2, P])
        less = sb("w_lss", [P, 4, 2 * HEADS])
        ex = sb("w_ex", [P, 4, 2, HEADS])
        rows = sb("w_rows", [P, 4, 2, wide])
        den = sb("w_dn", [P, 4, 2, HEADS])
        agg = sb("w_agg", [P, 4, 2, D])
        with nc.Block() as block:
            @block.sync
            def _(sp):
                def load(j, s):
                    if past(j, 4):
                        sp.wait_ge(S["turned"], ph.at("turned", j - 4))
                        sp.wait_ge(S["summed"], ph.at("summed", j - 4))
                    sp.dma_start(max_in[:, s, :, :].rearrange("h i p -> h (i p)"),
                                 m["max_line"][:, bass.ds(j * (2 * P), 2 * P)]).then_inc(S[f"others_in{s}"], 16)
                    sp.dma_start(v_in[:, s, :, :], m["v_tab"].rearrange("(t p) c -> p t c", p=P)[:, bass.ds(j * 2, 2), :]
                                 ).then_inc(S[f"own_in{s}"], 16)
                    sp.dma_start(sums[:, s, :, :], m["sum_tab"][bass.ds(j * 2, 2), :, :].rearrange("t p f -> p t f")
                                 ).then_inc(S[f"sums_in{s}"], 16)

                def store(j, s):
                    sp.wait_ge(S["done"], ph.at("done", j))
                    sp.dma_start(m["agg_tab"].rearrange("(t p) c -> p t c", p=P)[:, bass.ds(j * 2, 2), :],
                                 agg[:, s, :, :]).then_inc(S[f"stored{s}"], 16)
                skewed(sp, pairs, [(0, load), (5, store)])
                for s in range(4):
                    sp.wait_ge(S[f"stored{s}"], ph.ring_end("stored", s))

            @block.tensor
            def _(pe):
                def turn(j, s):
                    pool_wait(pe, S["ordered"], ph.at("ordered", j), S["apart"])
                    if past(j, 2):
                        pool_wait(pe, S["less"], ph.at("less", j - 2), S["apart"])
                    for i in range(2):
                        last = nc.tensor.transpose(psum[2 + s % 2][:, i * HEADS:(i + 1) * HEADS], ordered[:, s, i, :],
                                                   ident[0:HEADS, 0:HEADS])
                    last.then_inc(S["turned"], 1)

                def add_up(i):
                    def step(j, s):
                        pe.wait_ge(S["carried"], ph.at("carried", j, i + 1))
                        if i == 0:
                            pe.wait_ge(S[f"sums_in{s}"], ph.ring_at("sums_in", j, s))
                            if past(j, 2):
                                pe.wait_ge(S["done"], ph.at("done", j - 2))
                        nc.tensor.matmul(psum[s % 2][:, i * wide:(i + 1) * wide], sums[:, s, i, :], rows[:, s, i, :],
                                         start=True, stop=True).then_inc(S["summed"], 1)
                    return step
                skewed(pe, pairs, [(1, turn), (2, add_up(0)), (2, add_up(1))])

            @block.scalar
            def _(act):
                def weight(j, s):
                    act.wait_ge(S["less"], ph.at("less", j))
                    if past(j, 4):
                        act.wait_ge(S["weighed"], ph.at("weighed", j - 4))
                    nc.scalar.activation(ex[:, s, :, :].rearrange("p i h -> p (i h)"), less[:, s, :], ACT.Exp
                                         ).then_inc(S["exp"], 1)
                skewed(act, pairs, [(1, weight)])

            @block.vector
            def _(dve):
                def order(j, s):
                    dve.wait_ge(S[f"others_in{s}"], ph.ring_at("others_in", j, s))
                    if past(j, 4):
                        dve.wait_ge(S["turned"], ph.at("turned", j - 4))
                    v.tensor_copy(ordered[:, s, 0, :], max_in[:, s, 0, :])
                    v.tensor_copy(ordered[:, s, 1, :], max_in[:, s, 1, ::-1]).then_inc(S["ordered"], 1)

                def subtract(j, s):
                    dve.wait_ge(S["turned"], ph.at("turned", j))
                    if past(j, 4):
                        dve.wait_ge(S["exp"], ph.at("exp", j - 4))
                    v.tensor_tensor(less[:, s, :], m["alpha"][:, bass.ds(j * 2, 2), :].rearrange("p i h -> p (i h)"),
                                    psum[2 + s % 2][:, 0:2 * HEADS], ALU.subtract).then_inc(S["less"], 1)

                def weigh(j, s):
                    dve.wait_ge(S["exp"], ph.at("exp", j))
                    dve.wait_ge(S[f"own_in{s}"], ph.ring_at("own_in", j, s))
                    if past(j, 4):
                        dve.wait_ge(S["summed"], ph.at("summed", j - 4))
                    for i in range(2):
                        v.tensor_tensor(rows[:, s, i, 0:D].rearrange("p (h c) -> p h c", c=HC),
                                        v_in[:, s, i, :].rearrange("p (h c) -> p h c", c=HC),
                                        ex[:, s, i, :].unsqueeze(2).to_broadcast([P, HEADS, HC]), ALU.mult)
                    v.tensor_copy(rows[:, s, :, D:wide], ex[:, s, :, :]).then_inc(S["weighed"], 1)
                    dve.wait_ge(S["weighed"], ph.at("weighed", j))

                def carry_on(i):
                    p0 = (0, 96)[i]

                    def step(j, s):
                        if i == 0 and isinstance(j, int) and j == 0:
                            dve.sem_inc(S["carried"], 1)
                            return
                        if i == 0:
                            dve.wait_ge(S["summed"], ph.at("summed", j - 1))
                            before = psum[(s + 1) % 2][p0:p0 + 32, wide:2 * wide]
                        else:
                            dve.wait_ge(S["summed"], ph.at("summed", j, 1))
                            before = psum[s % 2][p0:p0 + 32, 0:wide]
                        v.scalar_tensor_tensor(rows[p0:p0 + 32, s, i, :], before,
                                               m["carry"][p0:p0 + 32, bass.ds(j * 2 + i, 1)],
                                               rows[p0:p0 + 32, s, i, :], ALU.mult, ALU.add
                                               ).then_inc(S["carried"], 1)
                    return step

                def divide(j, s):
                    dve.wait_ge(S["summed"], ph.at("summed", j))
                    if past(j, 4):
                        dve.wait_ge(S[f"stored{s}"], ph.ring_at("stored", j, s, back=1))
                    bank = psum[s % 2][:, 0:2 * wide].rearrange("p (i n) -> p i n", i=2)
                    v.tensor_scalar(den[:, s, :, :], bank[:, :, D:wide], DEN_EPS, None, ALU.add).then_inc(S["den"], 1)
                    dve.wait_ge(S["den"], ph.at("den", j, 1))
                    v.reciprocal(den[:, s, :, :], den[:, s, :, :]).then_inc(S["den"], 1)
                    dve.wait_ge(S["den"], ph.at("den", j, 2))
                    v.tensor_tensor(den[:, s, :, :], den[:, s, :, :],
                                    m["lead"][:, bass.ds(j * 2, 2)].unsqueeze(2).to_broadcast([P, 2, HEADS]),
                                    ALU.mult).then_inc(S["den"], 1)
                    dve.wait_ge(S["den"], ph.at("den", j, 3))
                    for i in range(2):
                        last = v.tensor_tensor(agg[:, s, i, :].rearrange("p (h c) -> p h c", c=HC),
                                               bank[:, i, 0:D].rearrange("p (h c) -> p h c", c=HC),
                                               den[:, s, i, :].unsqueeze(2).to_broadcast([P, HEADS, HC]), ALU.mult)
                    last.then_inc(S["done"], 1)
                skewed(dve, pairs, [(0, order), (2, weigh), (2, carry_on(0)), (1, subtract), (2, carry_on(1)),
                                    (3, divide)])


def finish(nc, S, counts, m, pairs, tile0, coupled):
    from contextlib import ExitStack
    ctx = ExitStack()

    def sb(name, shape, dt=F32):
        return ctx.enter_context(nc.sbuf_tensor(name, list(shape), dt))

    v, psum, ident = nc.vector, m["psum"], m["ident"]
    ph = counts.phase(pairs, {"own_in*": 16, "sums_in*": 16 if coupled else 0, "others_in*": 16, "turned": 1,
                              "copied": 1, "skip": 1, "skip_set": 1, "up": 1, "up_set": 1, "down": 1,
                              "down_set": 1, "sum": 1, "back": 1, "y": 1, "stats": 2, "var": 1,
                              "inverse": 1, "done": 1, "scattered*": 32})

    def past(j, n):
        return not isinstance(j, int) or j >= n

    tag = "fc_" if coupled else "fl_"
    with ctx:
        x_in = sb(tag + "x", [P, 4, 2, D])
        x_again = sb(tag + "x2", [P, 4, 2, D])
        agg = sb(tag + "agg", [P, 4, 2, D])
        xt = sb(tag + "xt", [P, 2, 2 * P])
        skip = sb(tag + "skip", [P, 4, 2 * P])
        up = sb(tag + "up", [P, 2, 2 * P])
        down = sb(tag + "down", [P, 2, 2 * P])
        total = sb(tag + "sum", [P, 2, 2 * P])
        y = sb(tag + "y", [P, 4, 2, D])
        stats = sb(tag + "stats", [P, 4, 2, 6])
        mv = sb(tag + "mv", [P, 4, 2, 2])
        var = sb(tag + "var", [P, 4, 2])
        inverse = sb(tag + "inv", [P, 4, 2])
        index = sb(tag + "idx", [P, 4, 2], I32)
        x1 = m["x1_tab"].rearrange("(t p) c -> p t c", p=P)
        with nc.Block() as block:
            @block.sync
            def _(sp):
                def load(j, s):
                    if past(j, 4):
                        sp.wait_ge(S["skip"], ph.at("skip", j - 4))
                    sp.dma_start(x_in[:, s, :, :], x1[:, bass.ds(j * 2 + tile0, 2), :]).then_inc(S[f"own_in{s}"], 16)
                    if coupled:
                        sp.dma_start(agg[:, s, :, :], m["agg_tab"].rearrange("(t p) c -> p t c", p=P)[
                            :, bass.ds(j * 2, 2), :]).then_inc(S[f"sums_in{s}"], 16)

                def load_again(j, s):
                    if past(j, 4):
                        sp.wait_ge(S["y"], ph.at("y", j - 4))
                    sp.dma_start(x_again[:, s, :, :], x1[:, bass.ds(j * 2 + tile0, 2), :]
                                 ).then_inc(S[f"others_in{s}"], 16)
                skewed(sp, pairs, [(0, load), (5, load_again)])

            @block.gpsimd
            def _(pool):
                def invert(j, s):
                    pool_wait(pool, S["var"], ph.at("var", j), S["apart"])
                    nc.gpsimd.tensor_tensor(inverse[:, s, :], var[:, s, :], m["neg_half"][:], ALU.pow
                                            ).then_inc(S["inverse"], 1)

                def scatter(j, s):
                    pool_wait(pool, S["done"], ph.at("done", j), S["apart"])
                    for i in range(2):
                        pool.indirect_dma_start(
                            out=m["out"], in_=y[:, s, i, :], in_offset=None,
                            out_offset=bass.IndirectOffsetOnAxis(ap=index[:, s, i:i + 1], axis=0),
                            bounds_check=NODES - 1, oob_is_err=False).then_inc(S[f"scattered{s}"], 16)
                skewed(pool, pairs, [(5, invert), (6, scatter)])
                for s in range(4):
                    pool.wait_ge(S[f"scattered{s}"], ph.ring_end("scattered", s))

            @block.tensor
            def _(pe):
                def turn(j, s):
                    pe.wait_ge(S[f"own_in{s}"], ph.ring_at("own_in", j, s))
                    if past(j, 2):
                        pe.wait_ge(S["copied"], ph.at("copied", j - 2))
                    for i in range(2):
                        last = nc.tensor.transpose(psum[s % 2][:, i * P:(i + 1) * P], x_in[:, s, i, :], ident[:])
                    last.then_inc(S["turned"], 1)

                def skip_(j, s):
                    pe.wait_ge(S["copied"], ph.at("copied", j))
                    if past(j, 2):
                        pe.wait_ge(S["skip_set"], ph.at("skip_set", j - 2))
                    last = nc.tensor.matmul(psum[2 + s % 2][:, 0:2 * P], m["w_skip"][:], xt[:, s % 2, :],
                                            start=True, stop=not coupled)
                    if coupled:
                        pe.wait_ge(S[f"sums_in{s}"], ph.ring_at("sums_in", j, s))
                        for i in range(2):
                            last = nc.tensor.matmul(psum[2 + s % 2][:, i * P:(i + 1) * P], agg[:, s, i, :], ident[:],
                                                    start=False, stop=(i == 1))
                    last.then_inc(S["skip"], 1)

                def up_(j, s):
                    pe.wait_ge(S["skip_set"], ph.at("skip_set", j))
                    if past(j, 2):
                        pe.wait_ge(S["up_set"], ph.at("up_set", j - 2))
                    nc.tensor.matmul(psum[4 + s % 2][:, 0:2 * P], m["w_up"][:], skip[:, s, :], start=True, stop=True
                                     ).then_inc(S["up"], 1)

                def down_(j, s):
                    pe.wait_ge(S["up_set"], ph.at("up_set", j))
                    if past(j, 2):
                        pe.wait_ge(S["down_set"], ph.at("down_set", j - 2))
                        pe.wait_ge(S["y"], ph.at("y", j - 2))
                    nc.tensor.matmul(psum[6 + s % 2][:, 0:2 * P], m["w_down"][:], up[:, s % 2, :], start=True, stop=True
                                     ).then_inc(S["down"], 1)

                def back(j, s):
                    pe.wait_ge(S["sum"], ph.at("sum", j))
                    if past(j, 2):
                        pe.wait_ge(S["y"], ph.at("y", j - 2))
                    for i in range(2):
                        last = nc.tensor.transpose(psum[6 + s % 2][:, (2 + i) * P:(3 + i) * P],
                                                   total[:, s % 2, i * P:(i + 1) * P], ident[:])
                    last.then_inc(S["back"], 1)
                skewed(pe, pairs, [(0, turn), (1, skip_), (2, up_), (3, down_), (4, back)])

            @block.scalar
            def _(act):
                def skip_(j, s):
                    act.wait_ge(S["skip"], ph.at("skip", j))
                    nc.scalar.activation(skip[:, s, :], psum[2 + s % 2][:, 0:2 * P], ACT.Identity,
                                         bias=m["b_skip"][:]).then_inc(S["skip_set"], 1)

                def up_(j, s):
                    act.wait_ge(S["up"], ph.at("up", j))
                    if past(j, 2):
                        act.wait_ge(S["down"], ph.at("down", j - 2))
                    nc.scalar.activation(up[:, s % 2, :], psum[4 + s % 2][:, 0:2 * P], ACT.Gelu_apprx_tanh,
                                         bias=m["b_up"][:]).then_inc(S["up_set"], 1)

                def down_(j, s):
                    act.wait_ge(S["down"], ph.at("down", j))
                    if past(j, 2):
                        act.wait_ge(S["sum"], ph.at("sum", j - 2))
                    nc.scalar.activation(down[:, s % 2, :], psum[6 + s % 2][:, 0:2 * P], ACT.Gelu_apprx_tanh,
                                         bias=m["b_down"][:]).then_inc(S["down_set"], 1)
                skewed(act, pairs, [(1, skip_), (2, up_), (3, down_)])

            @block.vector
            def _(dve):
                def copy(j, s):
                    dve.wait_ge(S["turned"], ph.at("turned", j))
                    if past(j, 2):
                        dve.wait_ge(S["skip"], ph.at("skip", j - 2))
                    v.tensor_copy(xt[:, s % 2, :], psum[s % 2][:, 0:2 * P]).then_inc(S["copied"], 1)

                def add(j, s):
                    dve.wait_ge(S["down_set"], ph.at("down_set", j))
                    if past(j, 2):
                        dve.wait_ge(S["back"], ph.at("back", j - 2))
                    v.tensor_tensor(total[:, s % 2, :], skip[:, s, :], down[:, s % 2, :], ALU.add
                                    ).then_inc(S["sum"], 1)

                def norm(j, s):
                    dve.wait_ge(S["back"], ph.at("back", j))
                    dve.wait_ge(S[f"others_in{s}"], ph.ring_at("others_in", j, s))
                    if past(j, 4):
                        dve.wait_ge(S[f"scattered{s}"], ph.ring_at("scattered", j, s, back=1))
                    v.tensor_copy(index[:, s, :], m["node_of"][:, bass.ds(j * 2 + tile0, 2)])
                    v.tensor_tensor(y[:, s, :, :].rearrange("p i c -> p (i c)"), psum[6 + s % 2][:, 2 * P:4 * P],
                                    x_again[:, s, :, :].rearrange("p i c -> p (i c)"), ALU.add).then_inc(S["y"], 1)
                    dve.wait_ge(S["y"], ph.at("y", j))
                    for i in range(2):
                        last = v.bn_stats(stats[:, s, i, :], y[:, s, i, :])
                    last.then_inc(S["stats"], 1)
                    pool_wait(dve, S["stats"], ph.at("stats", j, 1), S["apart"])
                    for i in range(2):
                        last = v.bn_aggr(mv[:, s, i, :], stats[:, s, i, :])
                    last.then_inc(S["stats"], 1)
                    dve.wait_ge(S["stats"], ph.at("stats", j))
                    v.tensor_scalar(var[:, s, :], mv[:, s, :, 1], LN_EPS, None, ALU.add).then_inc(S["var"], 1)

                def scale(j, s):
                    dve.wait_ge(S["inverse"], ph.at("inverse", j))
                    for i in range(2):
                        last = v.tensor_scalar(y[:, s, i, :], y[:, s, i, :], mv[:, s, i, 0:1], inverse[:, s, i:i + 1],
                                               ALU.subtract, ALU.mult)
                    last.then_inc(S["done"], 1)
                skewed(dve, pairs, [(6, scale), (0, copy), (5, norm), (3, add)])


def kernel(**inputs):
    import numpy as np
    import concourse.bacc as bacc
    from concourse.bass_utils import run_bass_kernel_spmd

    def tiles(v, fill):
        v = np.concatenate([v, np.full((SLOTS - EDGES,) + v.shape[1:], fill, v.dtype)])
        v = v.reshape((TE, P) + v.shape[1:]).copy()
        v[1::2] = v[1::2, ::-1]
        return v

    src, dst = np.asarray(inputs["src"]), np.asarray(inputs["dst"])
    attr, x = np.asarray(inputs["edge_attr_32"]), np.asarray(inputs["x"])
    pad = np.full(SLOTS - EDGES, NPAD, dst.dtype)
    behind = np.concatenate([dst[1:], pad[:1]])
    arrays = {
        "src": tiles(src, 0).T, "dst": tiles(dst, NPAD).T, "dst_next": tiles(behind, NPAD).T,
        "dst_rows": tiles(dst, NPAD).reshape(-1),
        "dst_line": np.concatenate([np.full(1, -1, dst.dtype), dst, pad, np.full(1, -1, dst.dtype)]),
        "edge_attr": np.concatenate([tiles(attr, 0).reshape(SLOTS, ED), np.ones((SLOTS, 1), attr.dtype)], 1).T,
        "x": np.concatenate([x, np.zeros((NPAD - NODES, D), x.dtype)]),
    }
    for name, value in inputs.items():
        if name.startswith("L"):
            arrays[name] = np.asarray(value)
    arrays = {f"in_{n}": np.ascontiguousarray(v) for n, v in arrays.items()}

    nc = bacc.Bacc("TRN2", target_bir_lowering=False, num_devices=1)
    a = {n[3:]: nc.dram_tensor(n, v.shape, mybir.dt.from_np(v.dtype), kind="ExternalInput").ap()
         for n, v in arrays.items()}
    out = nc.dram_tensor("out_dram", [NODES, D], F32, kind="ExternalOutput").ap()
    gnn_kernel(nc, a, out)
    r = run_bass_kernel_spmd(nc, [arrays], core_ids=[0])
    return r.results[0]["out_dram"]
```
